# Optimizing a Trainium2 kernel written in Bass

```python
import numpy as np
import jax
import jax.numpy as jnp

def _softmax(x, axis=-1):
    return jax.nn.softmax(x, axis=axis)

def _gelu(x):
    return jax.nn.gelu(x, approximate=True)

def _silu(x):
    return jax.nn.silu(x)

def _sigmoid(x):
    return jax.nn.sigmoid(x)

def _layernorm(x, axis=-1, eps=1e-05):
    m = jnp.mean(x, axis=axis, keepdims=True)
    v = jnp.var(x, axis=axis, keepdims=True)
    return (x - m) / jnp.sqrt(v + eps)

def _scatter_add(tgt, idx, src, axis=0):
    return tgt.at[idx].add(src)

def _segment_sum(src, seg, n):
    return jax.ops.segment_sum(src, seg, n)
kernel_name = 'mk_adaln_attn_ffn_d1_seqx_r8_47e517'

def setup_inputs(seed: int=0):
    np.random.seed(seed)
    _w = jnp.asarray

    def _rec_inputs():
        import jax
        import jax.numpy as jnp
        _rk = jax.random.key(seed)
        x = -0.000125 + 0.9999 * jax.random.normal(jax.random.fold_in(_rk, 1), (4, 256, 256), jnp.float32)
        _lenS = 256 - jax.random.randint(jax.random.fold_in(_rk, 7), (4,), 0, max(1, 256 // 4) + 1, jnp.int32)
        _lenS2 = 256 - jax.random.randint(jax.random.fold_in(_rk, 8), (4,), 0, max(1, 256 // 4) + 1, jnp.int32)
        fside_BxSxS_0 = -1.52775e-05 + 0.999936 * jax.random.normal(jax.random.fold_in(_rk, 11), (4, 256, 256), jnp.float32)
        cond_512 = -5.03954e-05 + 1.00559 * jax.random.normal(jax.random.fold_in(_rk, 12), (4, 64), jnp.float32)
        return (x, fside_BxSxS_0, cond_512)
    x, fside_BxSxS_0, cond_512 = _rec_inputs()

    def _L0_cond_setup():
        import jax, jax.numpy as jnp
        from jax import lax
        import numpy as np
        B, T, C, TD = (8, 256, 256, 64)

        def _bi_wkv(r, k, v, w, u, time_emb):
            tf = jax.nn.sigmoid(jnp.sum(time_emb, axis=-1))[:, None, None]
            decay = jnp.exp(-jnp.exp(w.astype(jnp.float32)))[None, :] * (0.5 + 0.5 * tf[:, :, 0])
            kf = k.astype(jnp.float32)
            vf = v.astype(jnp.float32)
            ek = jnp.exp(jnp.minimum(kf, 30.0))
            ekv = ek * vf

            def step(carry, x):
                a, b = carry
                ekv_t, ek_t = x
                a = a * decay + ekv_t
                b = b * decay + ek_t
                return ((a, b), (a, b))
            ekv_t = jnp.swapaxes(ekv, 0, 1)
            ek_t = jnp.swapaxes(ek, 0, 1)
            init = (jnp.zeros_like(decay), jnp.zeros_like(decay))
            _, (nf, df) = lax.scan(step, init, (ekv_t, ek_t))
            _, (nb, db) = lax.scan(step, init, (ekv_t, ek_t), reverse=True)
            nf = jnp.swapaxes(nf, 0, 1)
            df = jnp.swapaxes(df, 0, 1)
            nb = jnp.swapaxes(nb, 0, 1)
            db = jnp.swapaxes(db, 0, 1)
            euk = jnp.exp(jnp.minimum(u.astype(jnp.float32)[None, None, :] + kf, 30.0))
            num = nf + nb - ekv + euk * vf
            den = df + db - ek + euk
            base = jax.nn.sigmoid(r.astype(jnp.float32)) * (num / jnp.maximum(den, 1e-08))
            out = base * (0.8 + 0.2 * tf)
            return out.astype(r.dtype)
        key = jax.random.key(seed)
        ks = jax.random.split(key, 6)
        return {'r': jax.random.normal(ks[0], (B, T, C), dtype=jnp.float32), 'k': jax.random.normal(ks[1], (B, T, C), dtype=jnp.float32), 'v': jax.random.normal(ks[2], (B, T, C), dtype=jnp.float32), 'w': jax.random.normal(ks[3], (C,), dtype=jnp.float32), 'u': jax.random.normal(ks[4], (C,), dtype=jnp.float32), 'time_emb': jax.random.normal(ks[5], (B, TD), dtype=jnp.float32)}
    _L0_cond_all = _L0_cond_setup()
    _L0_cond_in = {k: v for k, v in _L0_cond_all.items() if k in ('w', 'u')}
    del _L0_cond_all

    def _L0_attn_setup():
        import jax, jax.numpy as jnp
        import numpy as np
        key = jax.random.key(seed)
        ks = jax.random.split(key, 5)
        B, S, D = (1, 512, 256)
        H, Dh = (16, 128)
        scale = 1.0 / np.sqrt(D).astype(np.float32)
        return {'x': jax.random.normal(ks[0], (B, S, D), dtype=jnp.float32), 'W_K': jax.random.normal(ks[1], (H, Dh, D), dtype=jnp.float32) * scale, 'W_Q': jax.random.normal(ks[2], (H, Dh, D), dtype=jnp.float32) * scale, 'W_V': jax.random.normal(ks[3], (H, Dh, D), dtype=jnp.float32) * scale, 'W_O': jax.random.normal(ks[4], (D, H * Dh), dtype=jnp.float32) * scale}
    _L0_attn_all = _L0_attn_setup()
    _L0_attn_in = {k: v for k, v in _L0_attn_all.items() if k in ('W_K', 'W_Q', 'W_V', 'W_O')}
    del _L0_attn_all

    def _L0_cond2_setup():
        import jax, jax.numpy as jnp
        from jax import lax
        import numpy as np
        B, T, C, TD = (8, 256, 256, 64)

        def _bi_wkv(r, k, v, w, u, time_emb):
            tf = jax.nn.sigmoid(jnp.sum(time_emb, axis=-1))[:, None, None]
            decay = jnp.exp(-jnp.exp(w.astype(jnp.float32)))[None, :] * (0.5 + 0.5 * tf[:, :, 0])
            kf = k.astype(jnp.float32)
            vf = v.astype(jnp.float32)
            ek = jnp.exp(jnp.minimum(kf, 30.0))
            ekv = ek * vf

            def step(carry, x):
                a, b = carry
                ekv_t, ek_t = x
                a = a * decay + ekv_t
                b = b * decay + ek_t
                return ((a, b), (a, b))
            ekv_t = jnp.swapaxes(ekv, 0, 1)
            ek_t = jnp.swapaxes(ek, 0, 1)
            init = (jnp.zeros_like(decay), jnp.zeros_like(decay))
            _, (nf, df) = lax.scan(step, init, (ekv_t, ek_t))
            _, (nb, db) = lax.scan(step, init, (ekv_t, ek_t), reverse=True)
            nf = jnp.swapaxes(nf, 0, 1)
            df = jnp.swapaxes(df, 0, 1)
            nb = jnp.swapaxes(nb, 0, 1)
            db = jnp.swapaxes(db, 0, 1)
            euk = jnp.exp(jnp.minimum(u.astype(jnp.float32)[None, None, :] + kf, 30.0))
            num = nf + nb - ekv + euk * vf
            den = df + db - ek + euk
            base = jax.nn.sigmoid(r.astype(jnp.float32)) * (num / jnp.maximum(den, 1e-08))
            out = base * (0.8 + 0.2 * tf)
            return out.astype(r.dtype)
        key = jax.random.key(seed)
        ks = jax.random.split(key, 6)
        return {'r': jax.random.normal(ks[0], (B, T, C), dtype=jnp.float32), 'k': jax.random.normal(ks[1], (B, T, C), dtype=jnp.float32), 'v': jax.random.normal(ks[2], (B, T, C), dtype=jnp.float32), 'w': jax.random.normal(ks[3], (C,), dtype=jnp.float32), 'u': jax.random.normal(ks[4], (C,), dtype=jnp.float32), 'time_emb': jax.random.normal(ks[5], (B, TD), dtype=jnp.float32)}
    _L0_cond2_all = _L0_cond2_setup()
    _L0_cond2_in = {k: v for k, v in _L0_cond2_all.items() if k in ('w', 'u')}
    del _L0_cond2_all

    def _L0_ffn_setup():
        import jax, jax.numpy as jnp
        import numpy as np
        B, S, D, E, TOPK = (4, 256, 256, 8, 2)
        key = jax.random.key(seed)
        k1, k2, k3 = jax.random.split(key, 3)
        x = jax.random.normal(k1, (B, S, D), dtype=jnp.float32)
        gate_w = jax.random.normal(k2, (E, D), dtype=jnp.float32) * 0.02
        expert_w = jax.random.normal(k3, (E, D, D), dtype=jnp.float32) / np.sqrt(D)
        expert_b = jnp.zeros((E, D), dtype=jnp.float32)
        return {'x': x, 'gate_w': gate_w, 'expert_w': expert_w, 'expert_b': expert_b}
    _L0_ffn_all = _L0_ffn_setup()
    _L0_ffn_in = {k: v for k, v in _L0_ffn_all.items() if k in ('gate_w', 'expert_w', 'expert_b')}
    del _L0_ffn_all
    return {'x': x, 'fside_BxSxS_0': fside_BxSxS_0, 'cond_512': cond_512, 'L0_cond_w': _L0_cond_in['w'], 'L0_cond_u': _L0_cond_in['u'], 'L0_attn_W_K': _L0_attn_in['W_K'], 'L0_attn_W_Q': _L0_attn_in['W_Q'], 'L0_attn_W_V': _L0_attn_in['W_V'], 'L0_attn_W_O': _L0_attn_in['W_O'], 'L0_cond2_w': _L0_cond2_in['w'], 'L0_cond2_u': _L0_cond2_in['u'], 'L0_ffn_gate_w': _L0_ffn_in['gate_w'], 'L0_ffn_expert_w': _L0_ffn_in['expert_w'], 'L0_ffn_expert_b': _L0_ffn_in['expert_b']}

def reference(x, fside_BxSxS_0, cond_512, L0_cond_w, L0_cond_u, L0_attn_W_K, L0_attn_W_Q, L0_attn_W_V, L0_attn_W_O, L0_cond2_w, L0_cond2_u, L0_ffn_gate_w, L0_ffn_expert_w, L0_ffn_expert_b):
    import jax
    import jax.numpy as jnp

    def _L0_cond_ref(r, k, v, w, u, time_emb):
        import jax, jax.numpy as jnp
        from jax import lax
        import numpy as np
        B, T, C, TD = (8, 256, 256, 64)

        def _bi_wkv(r, k, v, w, u, time_emb):
            tf = jax.nn.sigmoid(jnp.sum(time_emb, axis=-1))[:, None, None]
            decay = jnp.exp(-jnp.exp(w.astype(jnp.float32)))[None, :] * (0.5 + 0.5 * tf[:, :, 0])
            kf = k.astype(jnp.float32)
            vf = v.astype(jnp.float32)
            ek = jnp.exp(jnp.minimum(kf, 30.0))
            ekv = ek * vf

            def step(carry, x):
                a, b = carry
                ekv_t, ek_t = x
                a = a * decay + ekv_t
                b = b * decay + ek_t
                return ((a, b), (a, b))
            ekv_t = jnp.swapaxes(ekv, 0, 1)
            ek_t = jnp.swapaxes(ek, 0, 1)
            init = (jnp.zeros_like(decay), jnp.zeros_like(decay))
            _, (nf, df) = lax.scan(step, init, (ekv_t, ek_t))
            _, (nb, db) = lax.scan(step, init, (ekv_t, ek_t), reverse=True)
            nf = jnp.swapaxes(nf, 0, 1)
            df = jnp.swapaxes(df, 0, 1)
            nb = jnp.swapaxes(nb, 0, 1)
            db = jnp.swapaxes(db, 0, 1)
            euk = jnp.exp(jnp.minimum(u.astype(jnp.float32)[None, None, :] + kf, 30.0))
            num = nf + nb - ekv + euk * vf
            den = df + db - ek + euk
            base = jax.nn.sigmoid(r.astype(jnp.float32)) * (num / jnp.maximum(den, 1e-08))
            out = base * (0.8 + 0.2 * tf)
            return out.astype(r.dtype)
        return _bi_wkv(r, k, v, w, u, time_emb)

    def _L0_attn_ref(x, W_K, W_Q, W_V, W_O):
        import jax, jax.numpy as jnp
        import numpy as np
        b, pos, d_model = x.shape
        d_head = W_K.shape[1]
        k = jnp.einsum('ihd,bpd->biph', W_K, x)
        q = jnp.einsum('ihd,bpd->biph', W_Q, x)
        v = jnp.einsum('ihd,bpd->biph', W_V, x)
        scores = jnp.einsum('biph,biqh->biqp', k, q)
        mask = jnp.tril(jnp.ones((pos, pos), dtype=x.dtype))
        masked = scores * mask - jnp.float32(10000000000.0) * (1.0 - mask)
        attn = jax.nn.softmax(masked / jnp.sqrt(jnp.float32(d_head)), axis=-1)
        z = jnp.einsum('biqp,biph->biqh', attn, v)
        z_flat = jnp.transpose(z, (0, 2, 1, 3)).reshape(b, pos, -1)
        out = jnp.einsum('df,bqf->bqd', W_O, z_flat)
        return out

    def _L0_cond2_ref(r, k, v, w, u, time_emb):
        import jax, jax.numpy as jnp
        from jax import lax
        import numpy as np
        B, T, C, TD = (8, 256, 256, 64)

        def _bi_wkv(r, k, v, w, u, time_emb):
            tf = jax.nn.sigmoid(jnp.sum(time_emb, axis=-1))[:, None, None]
            decay = jnp.exp(-jnp.exp(w.astype(jnp.float32)))[None, :] * (0.5 + 0.5 * tf[:, :, 0])
            kf = k.astype(jnp.float32)
            vf = v.astype(jnp.float32)
            ek = jnp.exp(jnp.minimum(kf, 30.0))
            ekv = ek * vf

            def step(carry, x):
                a, b = carry
                ekv_t, ek_t = x
                a = a * decay + ekv_t
                b = b * decay + ek_t
                return ((a, b), (a, b))
            ekv_t = jnp.swapaxes(ekv, 0, 1)
            ek_t = jnp.swapaxes(ek, 0, 1)
            init = (jnp.zeros_like(decay), jnp.zeros_like(decay))
            _, (nf, df) = lax.scan(step, init, (ekv_t, ek_t))
            _, (nb, db) = lax.scan(step, init, (ekv_t, ek_t), reverse=True)
            nf = jnp.swapaxes(nf, 0, 1)
            df = jnp.swapaxes(df, 0, 1)
            nb = jnp.swapaxes(nb, 0, 1)
            db = jnp.swapaxes(db, 0, 1)
            euk = jnp.exp(jnp.minimum(u.astype(jnp.float32)[None, None, :] + kf, 30.0))
            num = nf + nb - ekv + euk * vf
            den = df + db - ek + euk
            base = jax.nn.sigmoid(r.astype(jnp.float32)) * (num / jnp.maximum(den, 1e-08))
            out = base * (0.8 + 0.2 * tf)
            return out.astype(r.dtype)
        return _bi_wkv(r, k, v, w, u, time_emb)

    def _L0_ffn_ref(x, gate_w, expert_w, expert_b):
        import jax, jax.numpy as jnp
        import numpy as np
        B, S, D, E, TOPK = (4, 256, 256, 8, 2)
        batch_shape = x.shape[:-1]
        xf = x.reshape(-1, x.shape[-1])
        T = xf.shape[0]
        logits = jnp.einsum('td,ed->te', xf, gate_w)
        top_w, top_i = jax.lax.top_k(logits, TOPK)
        top_w = jax.nn.softmax(top_w.astype(jnp.float32), axis=-1).astype(x.dtype)
        gates = jnp.zeros((T, logits.shape[-1]), dtype=x.dtype)
        gates = gates.at[jnp.arange(T)[:, None], top_i].set(top_w)
        y = jnp.einsum('td,edo->eto', xf, expert_w) + expert_b[:, None, :]
        out = jnp.einsum('te,eto->to', gates, y)
        return out.reshape(*batch_shape, -1)
    x = x + _L0_attn_ref(_L0_cond_ref(x, fside_BxSxS_0, fside_BxSxS_0, L0_cond_w, L0_cond_u, cond_512), L0_attn_W_K, L0_attn_W_Q, L0_attn_W_V, L0_attn_W_O)
    x = x + _L0_ffn_ref(_L0_cond2_ref(x, fside_BxSxS_0, fside_BxSxS_0, L0_cond2_w, L0_cond2_u, cond_512), L0_ffn_gate_w, L0_ffn_expert_w, L0_ffn_expert_b)
    return x

_drawn_inputs = setup_inputs


def setup_inputs(seed=0):
    import zlib

    import numpy as np

    out = dict(_drawn_inputs(seed))
    spreads = {'L0_ffn_expert_b': (0.0, 0.1)}
    factors = {}
    for name, (base, spread) in spreads.items():
        noise = np.random.default_rng([zlib.crc32(name.encode()), seed]).standard_normal(out[name].shape)
        drawn = base * np.exp(spread * noise) if base else spread * noise
        out[name] = jnp.asarray(drawn.astype(out[name].dtype))
    for name, factor in factors.items():
        out[name] = (out[name] * factor).astype(out[name].dtype)
    return out
```

```python
import concourse.bass as bass
import concourse.mybir as mybir
from concourse.alu_op_type import AluOpType as ALU

ACT = mybir.ActivationFunctionType
AX = mybir.AxisListType
F32, F32R, F16 = mybir.dt.float32, mybir.dt.float32r, mybir.dt.float16
BF16, U32 = mybir.dt.bfloat16, mybir.dt.uint32

P = 128
B, T, C = 4, 256, 256
TD = 64
H, DH = 16, 128
E = 8
CB = C // P
N = B * T
PAIR = 2 * T
NPAIR = B // 2
GROUPS, GH = 4, 4
HEADS = NPAIR * GH
TB = PAIR // P
SLOT = CB * GH * DH
SLOT_Q, SLOT_K, SLOT_V, SLOT_O = range(4)
EXPERT_SLOTS = (SLOT_V, SLOT_Q, SLOT_K, SLOT_O)
SCALE = float(DH) ** -0.5
MASKED = -1e10
LIFT = 2.0 ** 15

PROJ_AHEAD = TB + 2
PROJ_GROUP = HEADS * 2 + NPAIR * TB
UNITS_GROUP = HEADS * 2
ZO_GROUP = UNITS_GROUP + NPAIR * CB
COND1_DVE, COND1_ACT, COND1_POOL = 16, 4, 5
GATE_STEPS = 6 + 4 * TB
COND2_DVE, COND2_ACT, COND2_POOL = 15, 3, 5


def head_plan(group):
    values = [[], [], [0, 1], [2, 3]]
    proj, zo = 0, (2 + CB if group == "first" else 0)
    steps = []
    for p in range(NPAIR):
        for h in range(GH):
            last_pair = group == "last" and p == NPAIR - 1
            step = {"p": p, "h": h, "hd": p * GH + h}
            step["next_qk"] = not (last_pair and h == GH - 1)
            if step["next_qk"]:
                step["q"] = proj
                proj += 1
            step["v"] = []
            if not last_pair:
                for t in values[h]:
                    step["v"].append((t, proj))
                    proj += 1
            if step["next_qk"]:
                step["k"] = proj
                proj += 1
            step["o"] = []
            if h == 1 and not (group == "first" and p == 0):
                for c in range(CB):
                    step["o"].append((c, zo))
                    zo += 1
            step["prev"] = not (group == "first" and p == 0 and h == 0)
            step["z"] = [zo, zo + 1] if step["prev"] else []
            step["prev_h"], step["prev_p"] = (h - 1) % GH, p if h else 1 - p
            step["prev_units"] = [2 * step["hd"] - 2, 2 * step["hd"] - 1] if step["prev"] else []
            zo += len(step["z"])
            steps.append(step)
    return steps


FIRST, MIDDLE, LAST = head_plan("first"), head_plan("middle"), head_plan("last")
PROJ_TOTAL = PROJ_AHEAD + PROJ_GROUP * (GROUPS - 1) + max(s["k"] for s in LAST if s["next_qk"]) + 1


def zo_base(g):
    return ZO_GROUP * g - 2 - CB


ZO_UNITS = zo_base(GROUPS)
ZO_TOTAL = ZO_UNITS + 2
ZO_X0 = zo_base(GROUPS - 1) + LAST[GH + 1]["o"][-1][1] + 1


def proj_base(g):
    return PROJ_GROUP * g + PROJ_AHEAD


def last_event(plan, p, kind):
    return max(e for s in plan if s["p"] == p for _, e in s[kind])


def build(nc, ctx, ap):
    def sb(name, shape, dt):
        return ctx.enter_context(nc.sbuf_tensor(name, shape, dt))

    def sem(name):
        return ctx.enter_context(nc.semaphore(name))

    xT = sb("xT", [P, CB, N], F32)
    fT = sb("fT", [P, CB, N], F32)
    wu = sb("wu", [P, 4, CB], F32)
    temb = sb("temb", [P, B, TD], F32)
    gate_w = sb("gate_w", [P, CB, E], F32)
    expert_b = sb("expert_b", [E, C], F32)
    identf = sb("identf", [P, P], F32)
    ident16 = sb("ident16", [P, P], F16)
    identb = sb("identb", [P, P], BF16)
    negmask = sb("negmask", [P, P], BF16)
    iota = sb("iota", [P, E], F32)
    tsum = sb("tsum", [P, B], F32)
    tf = sb("tf", [P, B], F32)
    tdec = sb("tdec", [P, B], F32)
    tout = sb("tout", [P, B], F32)
    ew = sb("ew", [P, 2, CB], F32)
    decay = sb("decay", [P, 2, CB, B], F32)
    tiles = sb("tiles", [P, 2, 7, CB, T], F32)
    num2 = sb("num2", [P, CB, N], F32)
    den2 = sb("den2", [P, CB, N], F32)
    y_hi = sb("y_hi", [P, CB, N], F32R)
    y_lo = sb("y_lo", [P, CB, N], F32R)
    raw = sb("raw", [P, 4, CB, GH * DH], F32)
    w_hi = sb("w_hi", [P, 4, CB, GH * DH], F32R)
    w_lo = sb("w_lo", [P, 4, CB, GH * DH], F32R)
    qk_hi = sb("qk_hi", [P, 2, 2, PAIR], F32R)
    qk_lo = sb("qk_lo", [P, 2, 2, PAIR], F32R)
    v_hi = sb("v_hi", [P, NPAIR, TB, GH * DH], F32R)
    v_lo = sb("v_lo", [P, NPAIR, TB, GH * DH], F32R)
    top = sb("top", [P, 2, 2], F32)
    ntop = sb("ntop", [P, 2, 2], F32)
    ssum = sb("ssum", [P, 2, 2], F32)
    ssmall = sb("ssmall", [P, 2, 2], F32)
    rsum = sb("rsum", [P, 2, 2], F32)
    prob = sb("prob", [P, 2, 3 * P], F32)
    prob16 = sb("prob16", [P, 2, 2, 3 * P], F16)
    pT = sb("pT", [P, 2, 2, 4 * P], F32R)
    z_hi = sb("z_hi", [P, GH, PAIR], F32R)
    z_lo = sb("z_lo", [P, GH, PAIR], F32R)
    logit = sb("logit", [P, TB, E], F32)
    best = sb("best", [P, TB, E], F32)
    besti = sb("besti", [P, TB, E], U32)
    bestf = sb("bestf", [P, TB, E], F32)
    gap = sb("gap", [P, TB], F32)
    gw2 = sb("gw2", [P, TB], F32)
    gden = sb("gden", [P, TB], F32)
    gw1 = sb("gw1", [P, TB], F32)
    gsec = sb("gsec", [P, TB, E], F32)
    gates = sb("gates", [P, NPAIR, TB, E], F32)
    gatesT = tiles[0:E, 0, 2:2 + NPAIR].rearrange("e p c n -> e p (c n)")
    acc = fT[:, :, :].rearrange("p c (k o) -> p (c k) o", o=C)

    def ps(name, dt=F32):
        return ctx.enter_context(nc.psum_tensor(name, [P, 512 if dt == F32 else 1024], dt))

    psA = [ps("psA0"), ps("psA1")]
    psS = [ps("psS0"), ps("psS1")]
    psT = [ps("psT0", F16), ps("psT1", F16)]
    psZ = [ps("psZ0"), ps("psZ1")]
    psE = [psZ[0][:, :], psZ[1][:, :], psT[0][:, :].bitcast(F32), psT[1][:, :].bitcast(F32)]

    in_small, in_f0, in_x0, in_f1, in_x1, in_late = (sem(f"in_{n}") for n in ("small", "f0", "x0", "f1", "x1", "late"))
    raw_v, raw_qk, raw_o = sem("raw_v"), sem("raw_qk"), sem("raw_o")
    consts = sem("consts")
    const_step = sem("const_step")
    pre_dve, pre_act = sem("pre_dve"), sem("pre_act")
    c1_dve, c1_act, c1_pool = ([sem(f"c1_{n}{k}") for k in range(2)] for n in ("dve", "act", "pool"))
    c2_dve, c2_act, c2_pool = sem("c2_dve"), sem("c2_act"), sem("c2_pool")
    yhi_done, ylo_done = sem("yhi_done"), sem("ylo_done")
    whi_v, whi_qk, whi_o = sem("whi_v"), sem("whi_qk"), sem("whi_o")
    wlo_v, wlo_qk, wlo_o = sem("wlo_v"), sem("wlo_qk"), sem("wlo_o")
    projected, proj_hi, proj_lo = sem("projected"), sem("proj_hi"), sem("proj_lo")
    scored, topped, ntopped, exped = sem("scored"), sem("topped"), sem("ntopped"), sem("exped")
    summed, recipd, halved_hi, halved = sem("summed"), sem("recipd"), sem("halved_hi"), sem("halved")
    transposed, pT_ready = sem("transposed"), sem("pT_ready")
    zo_done, z_hi_done, zo_read = sem("zo_done"), sem("z_hi_done"), sem("zo_read")
    e_exp, e_dve, y2f_done, y2hi_done, y2lo_done = (sem(n) for n in ("e_exp", "e_dve", "y2f_done", "y2hi_done", "y2lo_done"))
    logits_done, gate_step, gap_exp, gates_done = (sem(n) for n in ("logits_done", "gate_step", "gap_exp", "gates_done"))
    gT_done, gT_copied, based, base_copied = (sem(n) for n in ("gT_done", "gT_copied", "based", "base_copied"))
    expert_done, expert_half, expert_read, stored = (sem(n) for n in ("expert_done", "expert_half", "expert_read", "stored"))

    block = ctx.enter_context(nc.Block())

    @block.sync
    def _(sp):
        sp.dma_start(wu[:], ap["wu"]).then_inc(in_small, 16)
        sp.dma_start(temb[:], ap["temb"].partition_broadcast(P)).then_inc(in_small, 16)
        sp.dma_start(fT[:, :, 0:PAIR], ap["fT"][:, :, 0:PAIR]).then_inc(in_f0, 16)
        sp.dma_start(xT[:, :, 0:PAIR], ap["xT"][:, :, 0:PAIR]).then_inc(in_x0, 16)

        def load(g):
            if g:
                sp.wait_ge(wlo_v, g)
            sp.dma_start(raw[:, SLOT_V], ap["weights"][g, :, SLOT_V]).then_inc(raw_v, 16)
            if g:
                sp.wait_ge(wlo_qk, g * GH)
            sp.dma_start(raw[:, SLOT_Q:SLOT_K + 1], ap["weights"][g, :, SLOT_Q:SLOT_K + 1]).then_inc(raw_qk, 16)
            if g:
                sp.wait_ge(wlo_o, g)
            sp.dma_start(raw[:, SLOT_O], ap["weights"][g, :, SLOT_O]).then_inc(raw_o, 16)

        load(0)
        sp.dma_start(fT[:, :, PAIR:N], ap["fT"][:, :, PAIR:N]).then_inc(in_f1, 16)
        sp.dma_start(xT[:, :, PAIR:N], ap["xT"][:, :, PAIR:N]).then_inc(in_x1, 16)
        sp.dma_start(gate_w[:], ap["gate_w"]).then_inc(in_late, 16)
        sp.dma_start(expert_b[:], ap["expert_b"]).then_inc(in_late, 16)
        for g in range(1, GROUPS + 1):
            load(g)
        for k in range(NPAIR * TB):
            sp.wait_ge(expert_read, (k // TB) * 4 * TB + 3 * TB + k % TB + 1)
            sp.dma_start(ap["out"][k * P:(k + 1) * P, :], acc[:, k, :]).then_inc(stored, 16)
        sp.wait_ge(stored, 16 * NPAIR * TB)

    EK, EUK, EKV, DF, DB, NF, NB = range(7)
    VCOPY = tiles[:, 1, 6]

    def keys(b):
        return fT[:, :, bass.ds(b * T, T)] if not isinstance(b, int) else fT[:, :, b * T:(b + 1) * T]

    def cols(t, b):
        return t[:, :, bass.ds(b * T, T)] if not isinstance(b, int) else t[:, :, b * T:(b + 1) * T]

    def col(t, b):
        return t[:, bass.ds(b, 1)] if not isinstance(b, int) else t[:, b:b + 1]

    def dec(w, c, b):
        d = decay[:, w, c]
        return (d[:, bass.ds(b, 1)] if not isinstance(b, int) else d[:, b:b + 1]).to_broadcast([P, T])

    def steps_of(b, w):
        if w == 0:
            k = b % 2
            n = b // 2
            return (lambda i: tiles[:, k, i]), (c1_dve[k], c1_act[k], c1_pool[k]), (n * COND1_DVE, n * COND1_ACT, n * COND1_POOL)
        return (lambda i: tiles[:, 0, i]), (c2_dve, c2_act, c2_pool), (b * COND2_DVE, b * COND2_ACT, b * COND2_POOL)

    def cond_dve(dve, b, w):
        tile, (done, act, pool), (d0, a0, p0) = steps_of(b, w)
        f = keys(b)
        if w == 0 and b >= 2:
            dve.wait_ge(done, d0)
            dve.wait_ge(act, a0)
            dve.wait_ge(pool, p0)
            dve.wait_ge(yhi_done, b - 1)
            dve.wait_ge(ylo_done, b - 1)
        if w == 1:
            dve.wait_ge(c1_dve[0], 2 * COND1_DVE)
            dve.wait_ge(c1_dve[1], 2 * COND1_DVE)
            dve.wait_ge(yhi_done, B)
            dve.wait_ge(ylo_done, B)
            if not isinstance(b, int) or b > 0:
                dve.wait_ge(done, d0)
                dve.wait_ge(pool, p0)
        if w == 0:
            dve.wait_ge(in_f0 if b < 2 else in_f1, 16)
        dve.tensor_scalar(tile(EK), f, 30.0, None, ALU.min).then_inc(done, 1)
        for c in range(CB):
            dve.tensor_scalar(tile(EUK)[:, c], f[:, c], wu[:, 2 * w + 1, c:c + 1], 30.0, ALU.add, ALU.min).then_inc(done, 1)
        yield
        dve.wait_ge(act, a0 + 1)
        for c in range(CB):
            dve.tensor_tensor_scan(tile(DF)[:, c], dec(w, c, b), tile(EK)[:, c], 0.0, ALU.mult, ALU.add).then_inc(done, 1)
        for c in range(CB):
            dve.tensor_tensor_scan(tile(DB)[:, c][:, ::-1], dec(w, c, b), tile(EK)[:, c][:, ::-1], 0.0, ALU.mult, ALU.add).then_inc(done, 1)
        yield
        dve.wait_ge(pool, p0 + 1)
        for c in range(CB):
            dve.tensor_tensor_scan(tile(NF)[:, c], dec(w, c, b), tile(EKV)[:, c], 0.0, ALU.mult, ALU.add).then_inc(done, 1)
        for c in range(CB):
            dve.tensor_tensor_scan(tile(NB)[:, c][:, ::-1], dec(w, c, b), tile(EKV)[:, c][:, ::-1], 0.0, ALU.mult, ALU.add).then_inc(done, 1)
        yield
        dve.wait_ge(done, d0 + 7)
        dve.tensor_tensor(tile(DF), tile(DF), tile(DB), ALU.add).then_inc(done, 1)
        dve.wait_ge(pool, p0 + 2)
        dve.wait_ge(done, d0 + 12)
        dve.tensor_tensor(tile(DF), tile(DF), tile(EUK), ALU.add).then_inc(done, 1)
        yield
        if w == 0:
            dve.wait_ge(act, a0 + 4)
            dve.wait_ge(done, d0 + 13)
            dve.scalar_tensor_tensor(tile(DF), tile(DF), 1e-8, tile(EK), ALU.max, ALU.mult).then_inc(done, 1)
            dve.wait_ge(done, d0 + 14)
            dve.reciprocal(tile(DB), tile(DF)).then_inc(done, 1)
            yield
            dve.wait_ge(done, d0 + 15)
            dve.wait_ge(pool, p0 + 5)
            dve.scalar_tensor_tensor(tile(NB), tile(NF), col(tout, b), tile(DB), ALU.mult, ALU.mult).then_inc(done, 1)
            yield
        else:
            dve.wait_ge(done, d0 + 13)
            dve.tensor_scalar(cols(den2, b), tile(DF), 1e-8, None, ALU.max).then_inc(done, 1)
            dve.wait_ge(pool, p0 + 5)
            dve.tensor_scalar(cols(num2, b), tile(NF), col(tout, b), None, ALU.mult).then_inc(done, 1)
            yield

    def cond_act(act, b, w):
        tile, (dve, done, pool), (d0, a0, p0) = steps_of(b, w)
        act.wait_ge(dve, d0 + 1)
        act.activation(tile(EK), tile(EK), ACT.Exp).then_inc(done, 1)
        if w == 1:
            act.activation(VCOPY, keys(b), ACT.Copy).then_inc(done, 1)
        act.wait_ge(dve, d0 + 3)
        act.activation(tile(EUK), tile(EUK), ACT.Exp).then_inc(done, 1)
        yield
        if w == 0:
            act.wait_ge(in_x0 if b < 2 else in_x1, 16)
            act.wait_ge(dve, d0 + 7)
            act.wait_ge(pool, p0 + 2)
            act.activation(tile(EK), cols(xT, b), ACT.Exp, scale=-1.0).then_inc(done, 1)
            act.wait_ge(done, a0 + 3)
            act.activation(tile(EK), tile(EK), ACT.Copy, bias=1.0).then_inc(done, 1)
            yield
            act.wait_ge(dve, d0 + COND1_DVE)
            act.activation(cols(y_hi, b), tile(NB), ACT.Copy).then_inc(yhi_done, 1)
            yield

    def cond_pool(pool, b, w):
        tile, (dve, act, done), (d0, a0, p0) = steps_of(b, w)
        f = keys(b) if w == 0 else VCOPY
        if w == 1:
            pool.wait_ge(act, a0 + 2)
        pool.wait_ge(act, a0 + 1)
        pool.tensor_tensor(tile(EKV), tile(EK), f, ALU.mult).then_inc(done, 1)
        pool.wait_ge(act, a0 + 2 + w)
        pool.tensor_tensor(tile(EUK), tile(EUK), tile(EK), ALU.subtract).then_inc(done, 1)
        yield
        pool.wait_ge(dve, d0 + 11)
        pool.tensor_tensor(tile(NF), tile(NF), tile(NB), ALU.add).then_inc(done, 1)
        pool.wait_ge(done, p0 + 2)
        pool.tensor_tensor(tile(EKV), tile(EUK), f, ALU.mult).then_inc(done, 1)
        pool.wait_ge(done, p0 + 4)
        pool.tensor_tensor(tile(NF), tile(NF), tile(EKV), ALU.add).then_inc(done, 1)
        yield
        if w == 0:
            pool.wait_ge(yhi_done, b + 1)
            pool.tensor_tensor(cols(y_lo, b), tile(NB), cols(y_hi, b).bitcast(F32), ALU.subtract).then_inc(ylo_done, 1)
            yield

    def y2_tile(b):
        return tiles[:, 1, b if b < 2 else b + 2]

    def y2_full(b):
        return tiles[:, 1, b + 2] if b < 2 else tiles[:, 0, b - 2]

    def weights_of(kind, h=None):
        if kind == "qk":
            return lambda t: t[:, SLOT_Q:SLOT_K + 1, :, h * DH:(h + 1) * DH]
        return lambda t: t[:, SLOT_V if kind == "v" else SLOT_O]

    @block.gpsimd
    def _(pool):
        pool.memset(identf[:], 0.0).then_inc(const_step, 1)
        pool.memset(ident16[:], 0.0).then_inc(const_step, 1)
        pool.memset(identb[:], 0.0).then_inc(const_step, 1)
        pool.memset(negmask[:], 0.0).then_inc(const_step, 1)
        pool.wait_ge(const_step, 4)
        for m in (identf, ident16, identb):
            pool.affine_select(out=m[:], in_=m[:], compare_op=ALU.not_equal, fill=1.0, base=0,
                               pattern=[[-1, P]], channel_multiplier=1).then_inc(consts, 1)
        pool.affine_select(out=negmask[:], in_=negmask[:], compare_op=ALU.is_ge, fill=MASKED, base=0,
                           pattern=[[-1, P]], channel_multiplier=1).then_inc(consts, 1)
        for e in range(E):
            pool.memset(iota[:, e:e + 1], float(e)).then_inc(consts, 1)

        def refill(kind, g, h=None):
            view = weights_of(kind, h)
            hi, lo = {"v": (whi_v, wlo_v), "qk": (whi_qk, wlo_qk), "o": (whi_o, wlo_o)}[kind]
            pool.wait_ge(hi, (g * GH + h if kind == "qk" else g) + 1)
            pool.tensor_tensor(view(w_lo), view(raw), view(w_hi).bitcast(F32), ALU.subtract).then_inc(lo, 1)

        c = [cond_pool(pool, b, 0) for b in range(B)]
        next(c[0])
        next(c[1])
        refill("v", 0)
        next(c[0])
        next(c[0])
        next(c[1])
        refill("qk", 0, 0)
        next(c[1])
        for h in range(1, GH):
            refill("qk", 0, h)

        def group(g):
            if isinstance(g, int) and g == 0:
                for b in (2, 3, 2, 2, 3, 3):
                    next(c[b])
            else:
                for _ in cond_pool(pool, g, 1):
                    pass
            refill("o", g)
            refill("v", g + 1)
            refill("qk", g + 1, 0)
            refill("qk", g + 1, 1)
            if isinstance(g, int) and g == 0:
                for _ in cond_pool(pool, 0, 1):
                    pass
            refill("qk", g + 1, 2)
            refill("qk", g + 1, 3)

        group(0)
        with pool.Fori(1, GROUPS) as g:
            group(g)
        refill("o", GROUPS)

    @block.scalar
    def _(act):
        act.wait_ge(in_small, 32)
        act.activation(ew[:], wu[:, 0:4:2], ACT.Exp).then_inc(pre_act, 1)
        act.wait_ge(pre_act, 1)
        act.activation(ew[:], ew[:], ACT.Exp, scale=-1.0).then_inc(pre_act, 1)
        act.wait_ge(pre_dve, 1)
        act.activation(tf[:], tsum[:], ACT.Exp, scale=-1.0).then_inc(pre_act, 1)

        def refill(kind, g, h=None, freed=None):
            view = weights_of(kind, h)
            landed, hi = {"v": (raw_v, whi_v), "qk": (raw_qk, whi_qk), "o": (raw_o, whi_o)}[kind]
            act.wait_ge(landed, g * 16 + 16)
            if freed is not None:
                act.wait_ge(*freed)
            act.activation(view(w_hi), view(raw), ACT.Copy).then_inc(hi, 1)

        def project_hi(out, i, bank):
            act.wait_ge(projected, i + 1)
            act.activation(out, psA[bank][:], ACT.Copy).then_inc(proj_hi, 1)

        c = [cond_act(act, b, 0) for b in range(B)]
        next(c[0])
        next(c[1])
        refill("v", 0)
        next(c[0])
        refill("qk", 0, 0)
        next(c[1])
        for h in range(1, GH):
            refill("qk", 0, h)
        next(c[0])
        refill("o", 0)
        next(c[1])
        for t in range(TB):
            project_hi(v_hi[:, 0, t], t, t % 2)
        project_hi(qk_hi[:, 0, 0], TB, 0)
        project_hi(qk_hi[:, 0, 1], TB + 1, 1)

        def transposed_copy(g, k):
            act.wait_ge(transposed, g * UNITS_GROUP + k + 1)
            act.activation(pT[:, k % 2, :, P:4 * P], psT[k % 2][:, 0:6 * P].rearrange("p (a n) -> p a n", a=2),
                           ACT.Copy).then_inc(pT_ready, 1)

        def z_high(h, k, i):
            act.wait_ge(zo_done, i + 1)
            act.activation(z_hi[:, h, (k % 2) * T:(k % 2) * T + T], psZ[k % 2][:, 0:T], ACT.Copy,
                           scale=1.0 / LIFT).then_inc(z_hi_done, 1)

        def group(g, plan, extra):
            for s in plan:
                hd, par = s["hd"], (s["hd"] + 1) % 2
                act.wait_ge(ntopped, g * HEADS + hd + 1)
                for k in (0, 1):
                    act.activation(prob[:, k, 0:P], psS[k][:, 0:P], ACT.Exp, scale=SCALE,
                                   bias=ntop[:, k, 0:1], accum_out=ssum[:, k, 0:1])
                    act.activation(prob[:, k, P:3 * P], psS[k][:, 2 * P:4 * P], ACT.Exp, scale=SCALE,
                                   bias=ntop[:, k, 1:2], accum_out=ssum[:, k, 1:2]).then_inc(exped, 1)
                if s["next_qk"]:
                    project_hi(qk_hi[:, par, 0], proj_base(g) + s["q"], s["q"] % 2)
                for k in s["prev_units"]:
                    transposed_copy(g, k)
                for f in extra.get((s["p"], s["h"], "a"), ()):
                    f()
                for t, i in s["v"]:
                    project_hi(v_hi[:, 1 - s["p"], t], proj_base(g) + i, i % 2)
                if s["next_qk"]:
                    project_hi(qk_hi[:, par, 1], proj_base(g) + s["k"], s["k"] % 2)
                for k, i in zip(s["prev_units"], s["z"]):
                    z_high(s["prev_h"], k, zo_base(g) + i)
                for f in extra.get((s["p"], s["h"], "c"), ()):
                    f()

        def extras(g, plan):
            first = isinstance(g, int) and g == 0
            c2 = cond_act(act, g, 1)
            out = {
                (1, 0, "a"): [lambda: refill("v", g + 1, freed=(projected, proj_base(g) + last_event(plan, 0, "v") + 1))],
                (1, 0, "c"): [lambda: refill("qk", g + 1, 0, (projected, proj_base(g) + plan[3]["k"] + 1))],
                (1, 1, "a"): [lambda: refill("qk", g + 1, 1, (projected, proj_base(g) + plan[4]["k"] + 1))],
                (1, 2, "a"): [lambda: refill("qk", g + 1, 2, (projected, proj_base(g) + plan[5]["k"] + 1))],
                (1, 3, "a"): [lambda: refill("qk", g + 1, 3, (projected, proj_base(g) + plan[6]["k"] + 1))],
            }
            if first:
                out[(0, 0, "a")] = [lambda: next(c[2]), lambda: next(c[3])]
                out[(0, 0, "c")] = [lambda: next(c[2])]
                out[(0, 1, "a")] = [lambda: next(c[3])]
                out[(0, 1, "c")] = [lambda: next(c[2])]
                out[(0, 2, "c")] = [lambda: next(c[3])]
                out[(1, 1, "c")] = [lambda: next(c2)]
            else:
                out[(0, 0, "c")] = [lambda: next(c2)]
                out[(0, 2, "a")] = [lambda: refill("o", g, freed=(zo_done, zo_base(g) + MIDDLE[1]["o"][-1][1] + 1))]
            if plan is LAST:
                out[(1, 1, "c")] = [lambda: y2_exp(0), lambda: y2_exp(1)]
                out[(1, 3, "c")] = [lambda: y2_hi(0), lambda: y2_hi(1)]
            return out

        def y2_exp(b):
            act.wait_ge(zo_read, ZO_X0 if b < 2 else ZO_TOTAL + CB)
            act.wait_ge(c2_dve, B * COND2_DVE)
            act.activation(y2_tile(b), cols(xT, b), ACT.Exp, scale=-1.0).then_inc(e_exp, 1)

        def y2_hi(b):
            act.wait_ge(y2f_done, b + 1)
            act.wait_ge(projected, proj_base(GROUPS - 1) + LAST[2]["k"] + 1 if b < 2 else PROJ_TOTAL)
            act.activation(cols(y_hi, b), y2_full(b), ACT.Copy).then_inc(y2hi_done, 1)

        group(0, FIRST, extras(0, FIRST))
        with act.Fori(1, GROUPS - 1) as g:
            group(g, MIDDLE, extras(g, MIDDLE))
        group(GROUPS - 1, LAST, extras(GROUPS - 1, LAST))
        for k in (-2, -1):
            transposed_copy(GROUPS, k)
        for k in (0, 1):
            z_high(GH - 1, k, ZO_UNITS + k)

        def gate_exp(p):
            act.wait_ge(gate_step, p * GATE_STEPS + 2 + 2 * TB)
            act.activation(gw2[:], gap[:], ACT.Exp).then_inc(gap_exp, 1)

        def copies(p):
            act.wait_ge(gT_done, p + 1)
            act.activation(gatesT[:, p], psS[1][0:E, :], ACT.Copy).then_inc(gT_copied, 1)
            for k in range(2):
                act.wait_ge(based, 2 * p + k + 1)
                act.activation(acc[:, p * TB + 2 * k:p * TB + 2 * k + 2],
                               psA[k][:].rearrange("p (a n) -> p a n", a=2), ACT.Copy).then_inc(base_copied, 1)

        gate_exp(0)
        refill("o", GROUPS, freed=(zo_done, ZO_TOTAL + CB))
        for b in range(2, 4):
            y2_exp(b)
        copies(0)
        for b in range(2, 4):
            y2_hi(b)
        gate_exp(1)
        copies(1)

    @block.vector
    def _(dve):
        dve.wait_ge(in_small, 32)
        dve.tensor_reduce(tsum[:], temb[:], AX.X, ALU.add).then_inc(pre_dve, 1)
        dve.wait_ge(pre_act, 3)
        dve.tensor_scalar(tf[:], tf[:], 1.0, None, ALU.add).then_inc(pre_dve, 1)
        dve.wait_ge(pre_dve, 2)
        dve.reciprocal(tf[:], tf[:]).then_inc(pre_dve, 1)
        dve.wait_ge(pre_dve, 3)
        dve.tensor_scalar(tdec[:], tf[:], 0.5, 0.5, ALU.mult, ALU.add).then_inc(pre_dve, 1)
        dve.tensor_scalar(tout[:], tf[:], 0.2, 0.8, ALU.mult, ALU.add).then_inc(pre_dve, 1)
        dve.wait_ge(pre_dve, 5)
        for w in range(2):
            for c in range(CB):
                dve.tensor_scalar(decay[:, w, c], tdec[:], ew[:, w, c:c + 1], None, ALU.mult).then_inc(pre_dve, 1)
        dve.memset(pT[:, :, :, 0:P].bitcast(F32), 0.0).then_inc(pre_dve, 1)
        dve.wait_ge(pre_dve, 10)

        def project_lo(out, hi, i, bank):
            dve.wait_ge(proj_hi, i + 1)
            dve.tensor_tensor(out, psA[bank][:], hi.bitcast(F32), ALU.subtract).then_inc(proj_lo, 1)

        c = [cond_dve(dve, b, 0) for b in range(B)]
        for b in (0, 1, 0, 1, 0, 0, 0, 1, 0, 1, 1, 1):
            next(c[b])
        for t in range(TB):
            project_lo(v_lo[:, 0, t], v_hi[:, 0, t], t, t % 2)
        for j in range(2):
            project_lo(qk_lo[:, 0, j], qk_hi[:, 0, j], TB + j, j)

        def maxima(g, hd):
            for k in (0, 1):
                dve.wait_ge(scored, g * UNITS_GROUP + 2 * hd + k + 1)
                dve.tensor_reduce(top[:, k, 0:1], psS[k][:, 0:P], AX.X, ALU.max).then_inc(topped, 1)
                dve.tensor_reduce(top[:, k, 1:2], psS[k][:, 2 * P:4 * P], AX.X, ALU.max).then_inc(topped, 1)
            dve.wait_ge(topped, 4 * (g * HEADS + hd + 1))
            dve.tensor_scalar(ntop[:], top[:], -SCALE, None, ALU.mult).then_inc(ntopped, 1)

        def sums(g, hd):
            n = g * HEADS + hd + 1
            dve.wait_ge(exped, 2 * n)
            dve.tensor_scalar(ssmall[:], ssum[:], 1.0 / LIFT, None, ALU.mult).then_inc(summed, 1)
            dve.wait_ge(summed, n)
            dve.reciprocal(rsum[:], ssmall[:]).then_inc(recipd, 1)

        def normalize(g, hd, k):
            n = g * UNITS_GROUP + 2 * hd + k
            if k == 0:
                dve.wait_ge(recipd, g * HEADS + hd + 1)
            if not (isinstance(g, int) and g == 0 and hd == 0):
                dve.wait_ge(transposed, n - 1)
            parts = [(slice(0, P), rsum[:, k, 0:1]), (slice(P, 3 * P), rsum[:, k, 1:2])]
            for c, r in parts:
                dve.tensor_scalar(prob16[:, k, 0, c], prob[:, k, c], r, None, ALU.mult).then_inc(halved_hi, 1)
            dve.wait_ge(halved_hi, 2 * n + 2)
            for c, r in parts:
                dve.scalar_tensor_tensor(prob16[:, k, 1, c], prob[:, k, c], r, prob16[:, k, 0, c],
                                         ALU.mult, ALU.subtract).then_inc(halved, 1)

        def add_output(p, c, i, bank):
            dve.wait_ge(zo_done, i + 1)
            dve.wait_ge(zo_read, i)
            x = xT[:, c, p * PAIR:(p + 1) * PAIR]
            dve.tensor_tensor(x, psZ[bank][:], x, ALU.add).then_inc(zo_read, 1)

        def z_low(h, g, k, i):
            dve.wait_ge(z_hi_done, g * UNITS_GROUP + k + 1)
            z = (slice(None), h, slice((k % 2) * T, (k % 2) * T + T))
            dve.scalar_tensor_tensor(z_lo[z], psZ[i % 2][:, 0:T], 1.0 / LIFT, z_hi[z].bitcast(F32),
                                     ALU.mult, ALU.subtract).then_inc(zo_read, 1)

        def group(g, plan, extra):
            for s in plan:
                hd, par = s["hd"], (s["hd"] + 1) % 2
                maxima(g, hd)
                if s["next_qk"]:
                    project_lo(qk_lo[:, par, 0], qk_hi[:, par, 0], proj_base(g) + s["q"], s["q"] % 2)
                sums(g, hd)
                normalize(g, hd, 0)
                for f in extra.get((s["p"], s["h"], "a"), ()):
                    f()
                for c, i in s["o"]:
                    add_output(1 - s["p"], c, zo_base(g) + i, i % 2)
                for t, i in s["v"]:
                    project_lo(v_lo[:, 1 - s["p"], t], v_hi[:, 1 - s["p"], t], proj_base(g) + i, i % 2)
                if s["next_qk"]:
                    project_lo(qk_lo[:, par, 1], qk_hi[:, par, 1], proj_base(g) + s["k"], s["k"] % 2)
                normalize(g, hd, 1)
                for k, i in zip(s["prev_units"], s["z"]):
                    z_low(s["prev_h"], g, k, zo_base(g) + i)
                for f in extra.get((s["p"], s["h"], "c"), ()):
                    f()

        def extras(g, plan):
            c2 = cond_dve(dve, g, 1)
            n2 = lambda: next(c2)
            if isinstance(g, int) and g == 0:
                n0, n1 = lambda: next(c[2]), lambda: next(c[3])
                out = {(0, 0, "a"): [n0, n1], (0, 0, "c"): [n0, n0, n0], (0, 1, "a"): [n1, n0], (0, 1, "c"): [n0, n1],
                       (0, 2, "a"): [n1, n1], (0, 2, "c"): [n1],
                       (1, 1, "a"): [n2], (1, 1, "c"): [n2], (1, 2, "a"): [n2], (1, 2, "c"): [n2], (1, 3, "c"): [n2]}
            else:
                out = {(0, 0, "a"): [n2], (0, 1, "a"): [n2], (0, 1, "c"): [n2], (0, 2, "c"): [n2], (0, 3, "c"): [n2]}
            if plan is LAST:
                out[(1, 2, "a")] = [lambda: y2_first(0)]
                out[(1, 2, "c")] = [lambda: y2_second(0), lambda: y2_first(1)]
                out[(1, 3, "a")] = [lambda: y2_second(1)]
                out[(1, 3, "c")] = [lambda: y2_lo(0), lambda: y2_lo(1)]
            return out

        def y2_first(b):
            dve.wait_ge(e_exp, b + 1)
            dve.scalar_tensor_tensor(y2_tile(b), y2_tile(b), 1.0, cols(den2, b), ALU.add, ALU.mult).then_inc(e_dve, 1)
            dve.wait_ge(e_dve, 2 * b + 1)
            dve.reciprocal(y2_tile(b), y2_tile(b)).then_inc(e_dve, 1)

        def y2_second(b):
            dve.wait_ge(e_dve, 2 * b + 2)
            dve.tensor_tensor(y2_full(b), y2_tile(b), cols(num2, b), ALU.mult).then_inc(y2f_done, 1)

        def y2_lo(b):
            dve.wait_ge(y2hi_done, b + 1)
            dve.tensor_tensor(cols(y_lo, b), y2_full(b), cols(y_hi, b).bitcast(F32), ALU.subtract).then_inc(y2lo_done, 1)

        group(0, FIRST, extras(0, FIRST))
        with dve.Fori(1, GROUPS - 1) as g:
            group(g, MIDDLE, extras(g, MIDDLE))
        group(GROUPS - 1, LAST, extras(GROUPS - 1, LAST))
        for k in (0, 1):
            z_low(GH - 1, GROUPS, k - 2, ZO_UNITS + k)

        def gate(p):
            n = [p * GATE_STEPS]

            def step(ins):
                n[0] += 1
                ins.then_inc(gate_step, 1)

            dve.wait_ge(logits_done, p + 1)
            if p:
                dve.wait_ge(gates_done, p)
            step(dve.tensor_copy(logit[:].rearrange("p t e -> p (t e)"), psS[0][:, p * 256:p * 256 + TB * E]))
            dve.wait_ge(gate_step, n[0])
            for t in range(TB):
                step(dve.max(best[:, t], logit[:, t]))
            dve.wait_ge(gate_step, n[0])
            for t in range(TB):
                step(dve.max_index(besti[:, t], best[:, t], logit[:, t]))
            step(dve.tensor_tensor(gap[:], best[:, :, 1], best[:, :, 0], ALU.subtract))
            dve.wait_ge(gate_step, n[0])
            step(dve.tensor_copy(bestf[:], besti[:]))
            dve.wait_ge(gap_exp, p + 1)
            step(dve.tensor_scalar(gden[:], gw2[:], 1.0, None, ALU.add))
            dve.wait_ge(gate_step, n[0])
            step(dve.reciprocal(gw1[:], gden[:]))
            dve.wait_ge(gate_step, n[0])
            step(dve.tensor_tensor(gw2[:], gw2[:], gw1[:], ALU.mult))
            dve.wait_ge(gate_step, n[0])
            for t in range(TB):
                step(dve.tensor_scalar(gates[:, p, t], iota[:], bestf[:, t, 0:1], gw1[:, t:t + 1], ALU.is_equal, ALU.mult))
                step(dve.tensor_scalar(gsec[:, t], iota[:], bestf[:, t, 1:2], gw2[:, t:t + 1], ALU.is_equal, ALU.mult))
            dve.wait_ge(gate_step, n[0])
            dve.tensor_tensor(gates[:, p], gates[:, p], gsec[:], ALU.add).then_inc(gates_done, 1)

        def add_experts(j):
            p, slot, t = j // (4 * TB), j // TB % 4, j % TB
            a = acc[:, p * TB + t]
            dve.wait_ge(base_copied, 2 * p + t // 2 + 1)
            dve.wait_ge(expert_done, j + 1)
            if slot:
                dve.wait_ge(expert_read, j - TB + 1)
            for e in range(2):
                if e:
                    dve.wait_ge(expert_half, j + 1)
                ins = dve.scalar_tensor_tensor(a, psE[j % 4][:, e * C:(e + 1) * C], gates[:, p, t, 2 * slot + e:2 * slot + e + 1],
                                               a, ALU.mult, ALU.add)
                ins.then_inc(expert_read if e else expert_half, 1)

        gate(0)
        for c in range(CB):
            add_output(1, c, ZO_TOTAL + c, c % 2)
        work = {2: [lambda: y2_first(2)], 5: [lambda: y2_second(2), lambda: y2_first(3)],
                8: [lambda: y2_second(3), lambda: y2_lo(2)], 9: [lambda: y2_lo(3)], 13: [lambda: gate(1)]}
        for j in range(8 * TB):
            add_experts(j)
            for f in work.get(j, ()):
                f()

    @block.tensor
    def _(pe):
        def three(out, pairs, start=True, stop=True):
            n = len(pairs)
            for k, ((ah, al), (bh, bl)) in enumerate(pairs):
                pe.matmul(out, ah, bh, start=start and k == 0, stop=False)
                pe.matmul(out, ah, bl, start=False, stop=False)
                ins = pe.matmul(out, al, bh, start=False, stop=stop and k == n - 1)
            return ins

        def both(hi, lo, *index):
            return hi[index], lo[index]

        def bank_free(i):
            if not (isinstance(i, int) and i < 2):
                pe.wait_ge(proj_lo, i - 1)

        def project_qk(j, h, p, i, bank):
            bank_free(i)
            three(psA[bank][:], [(both(w_hi, w_lo, slice(None), SLOT_Q + j, c, slice(h * DH, (h + 1) * DH)),
                                  both(y_hi, y_lo, slice(None), c, slice(p * PAIR, (p + 1) * PAIR)))
                                 for c in range(CB)]).then_inc(projected, 1)

        def project_v(t, p, i, bank):
            bank_free(i)
            k = p * PAIR + t * P
            three(psA[bank][:], [(both(y_hi, y_lo, slice(None), c, slice(k, k + P)),
                                  both(w_hi, w_lo, slice(None), SLOT_V, c)) for c in range(CB)]).then_inc(projected, 1)

        def scores(g, k, par):
            b = k % 2
            if not (isinstance(g, int) and g * UNITS_GROUP + k < 2):
                pe.wait_ge(exped, g * UNITS_GROUP + k - 1)
            for q in range(2):
                out, tokens = psS[b][:, q * T:(q + 1) * T], slice(b * T + q * P, b * T + q * P + P)
                keys_hi, keys_lo = (t[:, par, 1, b * T:(b + 1) * T] for t in (qk_hi, qk_lo))
                pe.matmul(out, qk_hi[:, par, 0, tokens], keys_hi, start=True, stop=False)
                pe.matmul(out, qk_hi[:, par, 0, tokens], keys_lo, start=False, stop=False)
                pe.matmul(out[:, q * P:(q + 1) * P], identb[:], negmask[:], start=False, stop=False)
                ins = pe.matmul(out, qk_lo[:, par, 0, tokens], keys_hi, start=False, stop=True)
            ins.then_inc(scored, 1)

        def transposes(g, k):
            u = k % 2
            pe.wait_ge(halved, 2 * (g * UNITS_GROUP + k + 1))
            if not (isinstance(g, int) and g * UNITS_GROUP + k < 2):
                pe.wait_ge(pT_ready, g * UNITS_GROUP + k - 1)
            for part in range(2):
                for n, c in enumerate((2, 0, 1)):
                    o = (part * 3 + n) * P
                    ins = pe.transpose(psT[u][:, o:o + P], prob16[:, u, part, c * P:(c + 1) * P], ident16[:])
            ins.then_inc(transposed, 1)

        def zo_free(i):
            if not (isinstance(i, int) and i < 2):
                pe.wait_ge(zo_read, i - 1)

        def values(g, k, h, p, i, bank):
            b = k % 2
            zo_free(i)
            pe.wait_ge(pT_ready, g * UNITS_GROUP + k + 1)
            three(psZ[bank][:, 0:T],
                  [(both(v_hi, v_lo, slice(None), p, 2 * b + kb, slice(h * DH, (h + 1) * DH)),
                    (pT[:, b, 0, (1 - kb) * T:(2 - kb) * T], pT[:, b, 1, (1 - kb) * T:(2 - kb) * T]))
                   for kb in range(2)]).then_inc(zo_done, 1)

        def output(c, i, bank):
            zo_free(i)
            pe.wait_ge(zo_read, i - c)
            three(psZ[bank][:], [(both(w_o_hi, w_o_lo, slice(None), h, slice(c * P, (c + 1) * P)),
                                  both(z_hi, z_lo, slice(None), h)) for h in range(GH)]).then_inc(zo_done, 1)

        w_o_hi = w_hi[:, SLOT_O].rearrange("p c n -> p (c n)").rearrange("p (h n) -> p h n", h=GH)
        w_o_lo = w_lo[:, SLOT_O].rearrange("p c n -> p (c n)").rearrange("p (h n) -> p h n", h=GH)

        pe.wait_ge(yhi_done, 2)
        pe.wait_ge(ylo_done, 2)
        pe.wait_ge(wlo_v, 1)
        for t in range(TB):
            project_v(t, 0, t, t % 2)
        pe.wait_ge(wlo_qk, 1)
        for j in range(2):
            project_qk(j, 0, 0, TB + j, j)
        pe.wait_ge(consts, 4 + E)
        pe.wait_ge(pre_dve, 10)

        def group(g, plan):
            for s in plan:
                p, h, par = s["p"], s["h"], s["hd"] % 2
                units = [2 * s["hd"], 2 * s["hd"] + 1]
                first = s["hd"] == 0
                k_event = proj_base(g) if first else proj_base(g) + plan[s["hd"] - 1]["k"] + 1
                pe.wait_ge(proj_lo, k_event)
                for k in units:
                    scores(g, k, par)
                nh, np_ = (h + 1) % GH, (p if h < GH - 1 else 1 - p)
                ng = g if s["hd"] < HEADS - 1 else g + 1
                if s["next_qk"]:
                    pe.wait_ge(wlo_qk, ng * GH + nh + 1)
                    if isinstance(g, int) and g == 0 and p == 0 and h == GH - 1:
                        pe.wait_ge(yhi_done, 4)
                        pe.wait_ge(ylo_done, 4)
                    project_qk(0, nh, np_, proj_base(g) + s["q"], s["q"] % 2)
                for k in s["prev_units"]:
                    transposes(g, k)
                for c, i in s["o"]:
                    pe.wait_ge(wlo_o, g + (1 if p == 1 else 0))
                    output(c, zo_base(g) + i, i % 2)
                for t, i in s["v"]:
                    if isinstance(g, int) and g == 0 and p == 0:
                        pe.wait_ge(yhi_done, 3 + t // 2)
                        pe.wait_ge(ylo_done, 3 + t // 2)
                    pe.wait_ge(wlo_v, g + 1 + p)
                    project_v(t, 1 - p, proj_base(g) + i, i % 2)
                if s["next_qk"]:
                    project_qk(1, nh, np_, proj_base(g) + s["k"], s["k"] % 2)
                for k, i in zip(s["prev_units"], s["z"]):
                    values(g, k, s["prev_h"], s["prev_p"], zo_base(g) + i, i % 2)

        group(0, FIRST)
        with pe.Fori(1, GROUPS - 1) as g:
            group(g, MIDDLE)
        group(GROUPS - 1, LAST)
        for k in (-2, -1):
            transposes(GROUPS, k)
        def logits(p):
            pe.wait_ge(y2f_done, 2 * p + 2)
            if p == 0:
                pe.wait_ge(exped, GROUPS * UNITS_GROUP)
            else:
                pe.wait_ge(gates_done, p)
            for t in range(TB):
                for c in range(CB):
                    k = (t % 2) * P
                    ins = pe.matmul(psS[0][:, p * 256 + t * E:p * 256 + (t + 1) * E], y2_full(2 * p + t // 2)[:, c, k:k + P],
                                    gate_w[:, c], start=c == 0, stop=c == CB - 1)
            ins.then_inc(logits_done, 1)

        def last_head():
            for k in (0, 1):
                values(GROUPS, k - 2, GH - 1, 1, ZO_UNITS + k, k)
            pe.wait_ge(wlo_o, GROUPS)
            for c in range(CB):
                output(c, ZO_TOTAL + c, c % 2)

        def gates_turn(p):
            pe.wait_ge(gates_done, p + 1)
            if p:
                pe.wait_ge(gT_copied, p)
            for t in range(TB):
                ins = pe.transpose(psS[1][0:E, t * P:(t + 1) * P], gates[:, p, t], identf[:])
            ins.then_inc(gT_done, 1)

        def base(p):
            pe.wait_ge(gT_copied, p + 1)
            if p:
                pe.wait_ge(base_copied, 2 * p)
            for k in range(2):
                for tt in range(2):
                    t = 2 * k + tt
                    n = p * PAIR + t * P
                    for c in range(CB):
                        o = psA[k][:, tt * C + c * P:tt * C + (c + 1) * P]
                        pe.matmul(o, gatesT[:, p, t * P:(t + 1) * P], expert_b[:, c * P:(c + 1) * P], start=True, stop=False)
                        ins = pe.matmul(o, xT[:, c, n:n + P], identf[:], start=False, stop=True)
                ins.then_inc(based, 1)

        def experts(j):
            p, slot, t = j // (4 * TB), j // TB % 4, j % TB
            if j >= 4:
                pe.wait_ge(expert_read, j - 3)
            elif j < 2:
                pe.wait_ge(zo_read, ZO_TOTAL + j + 1)
            else:
                pe.wait_ge(pT_ready, GROUPS * UNITS_GROUP)
            if j < 4 * TB:
                if slot == 0:
                    pe.wait_ge(wlo_v, GROUPS + 1)
                elif slot < 3:
                    pe.wait_ge(wlo_qk, (GROUPS + 1) * GH)
                else:
                    pe.wait_ge(wlo_o, GROUPS + 1)
            pe.wait_ge(y2lo_done, 2 * p + t // 2 + 1)
            n = p * PAIR + t * P
            three(psE[j % 4], [(both(y_hi, y_lo, slice(None), c, slice(n, n + P)),
                                both(w_hi, w_lo, slice(None), EXPERT_SLOTS[slot], c)) for c in range(CB)]).then_inc(expert_done, 1)

        pe.wait_ge(in_late, 32)
        logits(0)
        last_head()
        experts(0)
        gates_turn(0)
        experts(1)
        base(0)
        for j in range(2, 8 * TB):
            experts(j)
            if j == 12:
                logits(1)
            if j == 4 * TB + 1:
                gates_turn(1)
            if j == 4 * TB + 2:
                base(1)
    return None


def lay_out(inputs):
    import numpy as np

    def channels_first(a):
        return np.ascontiguousarray(a.reshape(N, CB, P).transpose(2, 1, 0))

    def by_channel(a):
        return a.reshape(a.shape[0], CB, P).transpose(2, 1, 0)

    weights = np.empty((GROUPS + 1, P, 4, CB, GH * DH), np.float32)
    for slot, name in ((SLOT_Q, "L0_attn_W_Q"), (SLOT_K, "L0_attn_W_K"), (SLOT_V, "L0_attn_W_V")):
        w = inputs[name]
        for g in range(GROUPS):
            weights[g, :, slot] = by_channel(w[g * GH:(g + 1) * GH].reshape(GH * DH, C))
    wo = inputs["L0_attn_W_O"].reshape(C, GROUPS, GH, DH).transpose(1, 3, 2, 0)
    weights[:GROUPS, :, SLOT_O] = wo.reshape(GROUPS, P, CB, GH * DH)
    we = inputs["L0_ffn_expert_w"].reshape(4, 2, CB, P, C).transpose(0, 3, 2, 1, 4)
    for k, slot in enumerate(EXPERT_SLOTS):
        weights[GROUPS, :, slot] = we[k].reshape(P, CB, GH * DH)
    wu = np.stack([inputs[n].reshape(CB, P).T for n in ("L0_cond_w", "L0_cond_u", "L0_cond2_w", "L0_cond2_u")], 1)
    return {
        "xT": channels_first(inputs["x"]),
        "fT": channels_first(inputs["fside_BxSxS_0"]),
        "temb": np.ascontiguousarray(inputs["cond_512"]),
        "wu": np.ascontiguousarray(wu),
        "weights": weights,
        "gate_w": np.ascontiguousarray(by_channel(inputs["L0_ffn_gate_w"])),
        "expert_b": np.ascontiguousarray(inputs["L0_ffn_expert_b"]),
    }


def kernel(**inputs):
    from contextlib import ExitStack
    import numpy as np
    import concourse.bacc as bacc
    from concourse.bass_utils import run_bass_kernel_spmd

    arrays = lay_out({k: np.asarray(v) for k, v in inputs.items()})
    nc = bacc.Bacc("TRN2", target_bir_lowering=False, num_devices=1)
    aps = {n: nc.dram_tensor("in_" + n, a.shape, F32, kind="ExternalInput").ap() for n, a in arrays.items()}
    aps["out"] = nc.dram_tensor("out", (N, C), F32, kind="ExternalOutput").ap()
    with ExitStack() as ctx:
        build(nc, ctx, aps)
    r = run_bass_kernel_spmd(nc, [{"in_" + n: a for n, a in arrays.items()}], core_ids=[0])
    return r.results[0]["out"].reshape(B, T, C)
```

```python
import concourse.bass as bass
import concourse.mybir as mybir
from concourse.alu_op_type import AluOpType as ALU

ACT = mybir.ActivationFunctionType
AX = mybir.AxisListType
F32, F32R, F16 = mybir.dt.float32, mybir.dt.float32r, mybir.dt.float16
BF16, U32 = mybir.dt.bfloat16, mybir.dt.uint32

P = 128
B, T, C = 4, 256, 256
TD = 64
H, DH = 16, 128
E = 8
CB = C // P
N = B * T
PAIR = 2 * T
NPAIR = B // 2
GROUPS, GH = 4, 4
HEADS = NPAIR * GH
TB = PAIR // P
SLOT = CB * GH * DH
SLOT_Q, SLOT_K, SLOT_V, SLOT_O = range(4)
EXPERT_SLOTS = (SLOT_V, SLOT_Q, SLOT_K, SLOT_O)
SCALE = float(DH) ** -0.5
MASKED = -1e10
LIFT = 2.0 ** 15

PROJ_AHEAD = TB + 2
PROJ_GROUP = HEADS * 2 + NPAIR * TB
UNITS_GROUP = HEADS * 2
ZO_GROUP = HEADS + NPAIR * CB
COND1_DVE, COND1_ACT, COND1_POOL = 16, 4, 5
GATE_STEPS = 6 + 4 * TB
COND2_DVE, COND2_ACT, COND2_POOL = 15, 3, 5


def head_plan(group):
    proj, zo = 0, (1 + CB if group == "first" else 0)
    steps = []
    for p in range(NPAIR):
        for h in range(GH):
            last_pair = group == "last" and p == NPAIR - 1
            step = {"p": p, "h": h, "hd": p * GH + h}
            step["next_qk"] = not (last_pair and h == GH - 1)
            if step["next_qk"]:
                step["q"] = proj
                proj += 1
                step["k"] = proj
                proj += 1
            step["v"] = []
            chunks = ([[], [], [0, 1], [2, 3]] if group == "first" else [[0], [], [1], [2, 3]]) if p == 0 else [[], [], [0, 1], [2, 3]]
            if not last_pair:
                for t in chunks[h]:
                    step["v"].append((t, proj))
                    proj += 1
            step["o"] = []
            if h == 1 and not (group == "first" and p == 0):
                for c in range(CB):
                    step["o"].append((c, zo))
                    zo += 1
            step["prev"] = not (group == "first" and p == 0 and h == 0)
            step["prev_h"], step["prev_p"] = (h - 1) % GH, p if h else 1 - p
            step["prev_units"] = [2 * step["hd"] - 2, 2 * step["hd"] - 1] if step["prev"] else []
            step["z"] = zo
            zo += step["prev"]
            steps.append(step)
    return steps


FIRST, MIDDLE, LAST = head_plan("first"), head_plan("middle"), head_plan("last")
PROJ_TOTAL = PROJ_AHEAD + PROJ_GROUP * (GROUPS - 1) + max(s["k"] for s in LAST if s["next_qk"]) + 1


def zo_base(g):
    return ZO_GROUP * g - 1 - CB


ZO_UNITS = zo_base(GROUPS)
ZO_TOTAL = ZO_UNITS + 1
ZO_X0 = zo_base(GROUPS - 1) + LAST[GH + 1]["o"][-1][1] + 1


def proj_base(g):
    return PROJ_GROUP * g + PROJ_AHEAD


def proj_bank(i):
    return i % 3


def zo_bank(i):
    return (i + zo_base(0)) % 2


def last_event(plan, p, kind):
    return max(e for s in plan if s["p"] == p for _, e in s[kind])


def build(nc, ctx, ap):
    def sb(name, shape, dt):
        return ctx.enter_context(nc.sbuf_tensor(name, shape, dt))

    def sem(name):
        return ctx.enter_context(nc.semaphore(name))

    xT = sb("xT", [P, CB, N], F32)
    fT = sb("fT", [P, CB, N], F32)
    wu = sb("wu", [P, 4, CB], F32)
    temb = sb("temb", [P, B, TD], F32)
    gate_w = sb("gate_w", [P, CB, E], F32)
    expert_b = sb("expert_b", [E, C], F32)
    identf = sb("identf", [P, P], F32)
    ident16 = sb("ident16", [P, P], F16)
    identb = sb("identb", [P, P], BF16)
    negmask = sb("negmask", [P, P], BF16)
    iota = sb("iota", [P, E], F32)
    tsum = sb("tsum", [P, B], F32)
    tf = sb("tf", [P, B], F32)
    tdec = sb("tdec", [P, B], F32)
    tout = sb("tout", [P, B], F32)
    ew = sb("ew", [P, 2, CB], F32)
    decay = sb("decay", [P, 2, CB, B], F32)
    tiles = sb("tiles", [P, 2, 7, CB, T], F32)
    num2 = sb("num2", [P, CB, N], F32)
    den2 = sb("den2", [P, CB, N], F32)
    y_hi = sb("y_hi", [P, CB, N], F32R)
    y_lo = sb("y_lo", [P, CB, N], F32R)
    raw = sb("raw", [P, 4, CB, GH * DH], F32)
    w_hi = sb("w_hi", [P, 4, CB, GH * DH], F32R)
    w_lo = sb("w_lo", [P, 4, CB, GH * DH], F32R)
    qk_hi = sb("qk_hi", [P, 2, 2, PAIR], F32R)
    qk_lo = sb("qk_lo", [P, 2, 2, PAIR], F32R)
    v_hi = sb("v_hi", [P, NPAIR, TB, GH * DH], F32R)
    v_lo = sb("v_lo", [P, NPAIR, TB, GH * DH], F32R)
    top = sb("top", [P, 2, 2], F32)
    ntop = sb("ntop", [P, 2, 2], F32)
    ssum = sb("ssum", [P, 2, 2], F32)
    ssmall = sb("ssmall", [P, 2, 2], F32)
    rsum = sb("rsum", [P, 2, 2], F32)
    prob = sb("prob", [P, 2, 3 * P], F32)
    prob16 = sb("prob16", [P, 2, 2, 3 * P], F16)
    pT = sb("pT", [P, 2, 2, 4 * P], F32R)
    z_hi = sb("z_hi", [P, GH, PAIR], F32R)
    z_lo = sb("z_lo", [P, GH, PAIR], F32R)
    logit = sb("logit", [P, TB, E], F32)
    best = sb("best", [P, TB, E], F32)
    besti = sb("besti", [P, TB, E], U32)
    bestf = sb("bestf", [P, TB, E], F32)
    gap = sb("gap", [P, TB], F32)
    gw2 = sb("gw2", [P, TB], F32)
    gden = sb("gden", [P, TB], F32)
    gw1 = sb("gw1", [P, TB], F32)
    gsec = sb("gsec", [P, TB, E], F32)
    gates = sb("gates", [P, NPAIR, TB, E], F32)
    gatesT = tiles[0:E, 0, 2:2 + NPAIR].rearrange("e p c n -> e p (c n)")
    acc = fT[:, :, :].rearrange("p c (k o) -> p (c k) o", o=C)

    def ps(name, dt=F32):
        return ctx.enter_context(nc.psum_tensor(name, [P, 512 if dt == F32 else 1024], dt))

    psA = [ps("psA0"), ps("psA1"), ps("psA2")]
    psS = [ps("psS0"), ps("psS1")]
    psT = ps("psT", F16)
    psZ = [ps("psZ0"), ps("psZ1")]
    psE = [psZ[0][:, :], psZ[1][:, :], psT[:, :].bitcast(F32), psA[2][:, :]]

    in_small, in_f0, in_x0, in_f1, in_x1, in_late = (sem(f"in_{n}") for n in ("small", "f0", "x0", "f1", "x1", "late"))
    raw_v, raw_qk, raw_o = sem("raw_v"), sem("raw_qk"), sem("raw_o")
    consts = sem("consts")
    const_step = sem("const_step")
    pre_dve, pre_act = sem("pre_dve"), sem("pre_act")
    c1_dve, c1_act, c1_pool = ([sem(f"c1_{n}{k}") for k in range(2)] for n in ("dve", "act", "pool"))
    c2_dve, c2_act, c2_pool = sem("c2_dve"), sem("c2_act"), sem("c2_pool")
    yhi_done, ylo_done = sem("yhi_done"), sem("ylo_done")
    whi_v, whi_qk, whi_o = sem("whi_v"), sem("whi_qk"), sem("whi_o")
    wlo_v, wlo_qk, wlo_o = sem("wlo_v"), sem("wlo_qk"), sem("wlo_o")
    projected, proj_hi, proj_lo = sem("projected"), sem("proj_hi"), sem("proj_lo")
    scored, topped, ntopped, exped = sem("scored"), sem("topped"), sem("ntopped"), sem("exped")
    summed, recipd, halved_hi, halved = sem("summed"), sem("recipd"), sem("halved_hi"), sem("halved")
    transposed, pT_ready = sem("transposed"), sem("pT_ready")
    zo_done, z_hi_done, zo_read = sem("zo_done"), sem("z_hi_done"), sem("zo_read")
    e_exp, e_dve, y2f_done, y2hi_done, y2lo_done = (sem(n) for n in ("e_exp", "e_dve", "y2f_done", "y2hi_done", "y2lo_done"))
    logits_done, gate_step, gap_exp, gates_done = (sem(n) for n in ("logits_done", "gate_step", "gap_exp", "gates_done"))
    gT_done, gT_copied, based, base_copied = (sem(n) for n in ("gT_done", "gT_copied", "based", "base_copied"))
    expert_done, expert_half, expert_read, stored = (sem(n) for n in ("expert_done", "expert_half", "expert_read", "stored"))

    block = ctx.enter_context(nc.Block())

    @block.sync
    def _(sp):
        sp.dma_start(wu[:], ap["wu"]).then_inc(in_small, 16)
        sp.dma_start(temb[:], ap["temb"].partition_broadcast(P)).then_inc(in_small, 16)
        sp.dma_start(fT[:, :, 0:PAIR], ap["fT"][:, :, 0:PAIR]).then_inc(in_f0, 16)
        sp.dma_start(xT[:, :, 0:PAIR], ap["xT"][:, :, 0:PAIR]).then_inc(in_x0, 16)

        def load(g):
            if g:
                sp.wait_ge(wlo_v, g)
            sp.dma_start(raw[:, SLOT_V], ap["weights"][g, :, SLOT_V]).then_inc(raw_v, 16)
            if g:
                sp.wait_ge(wlo_qk, g * GH)
            sp.dma_start(raw[:, SLOT_Q:SLOT_K + 1], ap["weights"][g, :, SLOT_Q:SLOT_K + 1]).then_inc(raw_qk, 16)
            if g:
                sp.wait_ge(wlo_o, g)
            sp.dma_start(raw[:, SLOT_O], ap["weights"][g, :, SLOT_O]).then_inc(raw_o, 16)

        load(0)
        sp.dma_start(fT[:, :, PAIR:N], ap["fT"][:, :, PAIR:N]).then_inc(in_f1, 16)
        sp.dma_start(xT[:, :, PAIR:N], ap["xT"][:, :, PAIR:N]).then_inc(in_x1, 16)
        sp.dma_start(gate_w[:], ap["gate_w"]).then_inc(in_late, 16)
        sp.dma_start(expert_b[:], ap["expert_b"]).then_inc(in_late, 16)
        for g in range(1, GROUPS + 1):
            load(g)
        for k in range(NPAIR * TB):
            sp.wait_ge(expert_read, (k // TB) * 4 * TB + 3 * TB + k % TB + 1)
            sp.dma_start(ap["out"][k * P:(k + 1) * P, :], acc[:, k, :]).then_inc(stored, 16)
        sp.wait_ge(stored, 16 * NPAIR * TB)

    EK, EUK, EKV, DF, DB, NF, NB = range(7)
    VCOPY = tiles[:, 1, 6]

    def keys(b):
        return fT[:, :, bass.ds(b * T, T)] if not isinstance(b, int) else fT[:, :, b * T:(b + 1) * T]

    def cols(t, b):
        return t[:, :, bass.ds(b * T, T)] if not isinstance(b, int) else t[:, :, b * T:(b + 1) * T]

    def col(t, b):
        return t[:, bass.ds(b, 1)] if not isinstance(b, int) else t[:, b:b + 1]

    def dec(w, c, b):
        d = decay[:, w, c]
        return (d[:, bass.ds(b, 1)] if not isinstance(b, int) else d[:, b:b + 1]).to_broadcast([P, T])

    def steps_of(b, w):
        if w == 0:
            k = b % 2
            n = b // 2
            return (lambda i: tiles[:, k, i]), (c1_dve[k], c1_act[k], c1_pool[k]), (n * COND1_DVE, n * COND1_ACT, n * COND1_POOL)
        return (lambda i: tiles[:, 0, i]), (c2_dve, c2_act, c2_pool), (b * COND2_DVE, b * COND2_ACT, b * COND2_POOL)

    def cond_dve(dve, b, w):
        tile, (done, act, pool), (d0, a0, p0) = steps_of(b, w)
        f = keys(b)
        if w == 0 and b >= 2:
            dve.wait_ge(done, d0)
            dve.wait_ge(act, a0)
            dve.wait_ge(pool, p0)
            dve.wait_ge(yhi_done, b - 1)
            dve.wait_ge(ylo_done, b - 1)
        if w == 1:
            dve.wait_ge(c1_dve[0], 2 * COND1_DVE)
            dve.wait_ge(c1_dve[1], 2 * COND1_DVE)
            dve.wait_ge(yhi_done, B)
            dve.wait_ge(ylo_done, B)
            if not isinstance(b, int) or b > 0:
                dve.wait_ge(done, d0)
                dve.wait_ge(pool, p0)
        if w == 0:
            dve.wait_ge(in_f0 if b < 2 else in_f1, 16)
        dve.tensor_scalar(tile(EK), f, 30.0, None, ALU.min).then_inc(done, 1)
        for c in range(CB):
            dve.tensor_scalar(tile(EUK)[:, c], f[:, c], wu[:, 2 * w + 1, c:c + 1], 30.0, ALU.add, ALU.min).then_inc(done, 1)
        yield
        dve.wait_ge(act, a0 + 1)
        for c in range(CB):
            dve.tensor_tensor_scan(tile(DF)[:, c], dec(w, c, b), tile(EK)[:, c], 0.0, ALU.mult, ALU.add).then_inc(done, 1)
        for c in range(CB):
            dve.tensor_tensor_scan(tile(DB)[:, c][:, ::-1], dec(w, c, b), tile(EK)[:, c][:, ::-1], 0.0, ALU.mult, ALU.add).then_inc(done, 1)
        yield
        dve.wait_ge(pool, p0 + 1)
        for c in range(CB):
            dve.tensor_tensor_scan(tile(NF)[:, c], dec(w, c, b), tile(EKV)[:, c], 0.0, ALU.mult, ALU.add).then_inc(done, 1)
        for c in range(CB):
            dve.tensor_tensor_scan(tile(NB)[:, c][:, ::-1], dec(w, c, b), tile(EKV)[:, c][:, ::-1], 0.0, ALU.mult, ALU.add).then_inc(done, 1)
        yield
        dve.wait_ge(done, d0 + 7)
        dve.tensor_tensor(tile(DF), tile(DF), tile(DB), ALU.add).then_inc(done, 1)
        dve.wait_ge(pool, p0 + 2)
        dve.wait_ge(done, d0 + 12)
        dve.tensor_tensor(tile(DF), tile(DF), tile(EUK), ALU.add).then_inc(done, 1)
        yield
        if w == 0:
            dve.wait_ge(act, a0 + 4)
            dve.wait_ge(done, d0 + 13)
            dve.scalar_tensor_tensor(tile(DF), tile(DF), 1e-8, tile(EK), ALU.max, ALU.mult).then_inc(done, 1)
            dve.wait_ge(done, d0 + 14)
            dve.reciprocal(tile(DB), tile(DF)).then_inc(done, 1)
            yield
            dve.wait_ge(done, d0 + 15)
            dve.wait_ge(pool, p0 + 5)
            dve.scalar_tensor_tensor(tile(NB), tile(NF), col(tout, b), tile(DB), ALU.mult, ALU.mult).then_inc(done, 1)
            yield
        else:
            dve.wait_ge(done, d0 + 13)
            dve.tensor_scalar(cols(den2, b), tile(DF), 1e-8, None, ALU.max).then_inc(done, 1)
            dve.wait_ge(pool, p0 + 5)
            dve.tensor_scalar(cols(num2, b), tile(NF), col(tout, b), None, ALU.mult).then_inc(done, 1)
            yield

    def cond_act(act, b, w):
        tile, (dve, done, pool), (d0, a0, p0) = steps_of(b, w)
        act.wait_ge(dve, d0 + 1)
        act.activation(tile(EK), tile(EK), ACT.Exp).then_inc(done, 1)
        if w == 1:
            act.activation(VCOPY, keys(b), ACT.Copy).then_inc(done, 1)
        act.wait_ge(dve, d0 + 3)
        act.activation(tile(EUK), tile(EUK), ACT.Exp).then_inc(done, 1)
        yield
        if w == 0:
            act.wait_ge(in_x0 if b < 2 else in_x1, 16)
            act.wait_ge(dve, d0 + 7)
            act.wait_ge(pool, p0 + 2)
            act.activation(tile(EK), cols(xT, b), ACT.Exp, scale=-1.0).then_inc(done, 1)
            act.wait_ge(done, a0 + 3)
            act.activation(tile(EK), tile(EK), ACT.Copy, bias=1.0).then_inc(done, 1)
            yield
            act.wait_ge(dve, d0 + COND1_DVE)
            act.activation(cols(y_hi, b), tile(NB), ACT.Copy).then_inc(yhi_done, 1)
            yield

    def cond_pool(pool, b, w):
        tile, (dve, act, done), (d0, a0, p0) = steps_of(b, w)
        f = keys(b) if w == 0 else VCOPY
        if w == 1:
            pool.wait_ge(act, a0 + 2)
        pool.wait_ge(act, a0 + 1)
        pool.tensor_tensor(tile(EKV), tile(EK), f, ALU.mult).then_inc(done, 1)
        pool.wait_ge(act, a0 + 2 + w)
        pool.tensor_tensor(tile(EUK), tile(EUK), tile(EK), ALU.subtract).then_inc(done, 1)
        yield
        pool.wait_ge(dve, d0 + 11)
        pool.tensor_tensor(tile(NF), tile(NF), tile(NB), ALU.add).then_inc(done, 1)
        pool.wait_ge(done, p0 + 2)
        pool.tensor_tensor(tile(EKV), tile(EUK), f, ALU.mult).then_inc(done, 1)
        pool.wait_ge(done, p0 + 4)
        pool.tensor_tensor(tile(NF), tile(NF), tile(EKV), ALU.add).then_inc(done, 1)
        yield
        if w == 0:
            pool.wait_ge(yhi_done, b + 1)
            pool.tensor_tensor(cols(y_lo, b), tile(NB), cols(y_hi, b).bitcast(F32), ALU.subtract).then_inc(ylo_done, 1)
            yield

    def y2_tile(b):
        return tiles[:, 1, b if b < 2 else b + 2]

    def y2_full(b):
        return tiles[:, 1, b + 2] if b < 2 else tiles[:, 0, b - 2]

    def weights_of(kind, h=None):
        if kind == "qk":
            return lambda t: t[:, SLOT_Q:SLOT_K + 1, :, h * DH:(h + 1) * DH]
        return lambda t: t[:, SLOT_V if kind == "v" else SLOT_O]

    @block.gpsimd
    def _(pool):
        pool.memset(identf[:], 0.0).then_inc(const_step, 1)
        pool.memset(ident16[:], 0.0).then_inc(const_step, 1)
        pool.memset(identb[:], 0.0).then_inc(const_step, 1)
        pool.memset(negmask[:], 0.0).then_inc(const_step, 1)
        pool.wait_ge(const_step, 4)
        for m in (identf, ident16, identb):
            pool.affine_select(out=m[:], in_=m[:], compare_op=ALU.not_equal, fill=1.0, base=0,
                               pattern=[[-1, P]], channel_multiplier=1).then_inc(consts, 1)
        pool.affine_select(out=negmask[:], in_=negmask[:], compare_op=ALU.is_ge, fill=MASKED, base=0,
                           pattern=[[-1, P]], channel_multiplier=1).then_inc(consts, 1)
        for e in range(E):
            pool.memset(iota[:, e:e + 1], float(e)).then_inc(consts, 1)

        def refill(kind, g, h=None):
            view = weights_of(kind, h)
            hi, lo = {"v": (whi_v, wlo_v), "qk": (whi_qk, wlo_qk), "o": (whi_o, wlo_o)}[kind]
            pool.wait_ge(hi, (g * GH + h if kind == "qk" else g) + 1)
            pool.tensor_tensor(view(w_lo), view(raw), view(w_hi).bitcast(F32), ALU.subtract).then_inc(lo, 1)

        c = [cond_pool(pool, b, 0) for b in range(B)]
        next(c[0])
        next(c[1])
        refill("v", 0)
        next(c[0])
        next(c[0])
        next(c[1])
        refill("qk", 0, 0)
        next(c[1])
        for h in range(1, GH):
            refill("qk", 0, h)

        def group(g):
            if isinstance(g, int) and g == 0:
                for b in (2, 3, 2, 2, 3, 3):
                    next(c[b])
            else:
                for _ in cond_pool(pool, g, 1):
                    pass
            refill("o", g)
            refill("v", g + 1)
            refill("qk", g + 1, 0)
            refill("qk", g + 1, 1)
            if isinstance(g, int) and g == 0:
                for _ in cond_pool(pool, 0, 1):
                    pass
            refill("qk", g + 1, 2)
            refill("qk", g + 1, 3)

        group(0)
        with pool.Fori(1, GROUPS) as g:
            group(g)
        refill("o", GROUPS)

    @block.scalar
    def _(act):
        act.wait_ge(in_small, 32)
        act.activation(ew[:], wu[:, 0:4:2], ACT.Exp).then_inc(pre_act, 1)
        act.wait_ge(pre_act, 1)
        act.activation(ew[:], ew[:], ACT.Exp, scale=-1.0).then_inc(pre_act, 1)
        act.wait_ge(pre_dve, 1)
        act.activation(tf[:], tsum[:], ACT.Exp, scale=-1.0).then_inc(pre_act, 1)

        def refill(kind, g, h=None, freed=None):
            view = weights_of(kind, h)
            landed, hi = {"v": (raw_v, whi_v), "qk": (raw_qk, whi_qk), "o": (raw_o, whi_o)}[kind]
            act.wait_ge(landed, g * 16 + 16)
            if freed is not None:
                act.wait_ge(*freed)
            act.activation(view(w_hi), view(raw), ACT.Copy).then_inc(hi, 1)

        def project_hi(out, i, bank):
            act.wait_ge(projected, i + 1)
            act.activation(out, psA[bank][:], ACT.Copy).then_inc(proj_hi, 1)

        c = [cond_act(act, b, 0) for b in range(B)]
        next(c[0])
        next(c[1])
        refill("v", 0)
        next(c[0])
        refill("qk", 0, 0)
        next(c[1])
        for h in range(1, GH):
            refill("qk", 0, h)
        next(c[0])
        refill("o", 0)
        next(c[1])
        for t in range(TB):
            project_hi(v_hi[:, 0, t], t, proj_bank(t))
        for j in range(2):
            project_hi(qk_hi[:, 0, j], TB + j, proj_bank(TB + j))

        def transposed_copy(g, k):
            act.wait_ge(transposed, g * UNITS_GROUP + k + 1)
            act.activation(pT[:, k % 2, :, P:4 * P], psT[:, 0:6 * P].rearrange("p (a n) -> p a n", a=2),
                           ACT.Copy).then_inc(pT_ready, 1)

        def z_high(h, i, bank):
            act.wait_ge(zo_done, i + 1)
            act.activation(z_hi[:, h], psZ[bank][:], ACT.Copy, scale=1.0 / LIFT).then_inc(z_hi_done, 1)

        def group(g, plan, extra):
            for s in plan:
                hd, par = s["hd"], (s["hd"] + 1) % 2
                if s["prev"]:
                    transposed_copy(g, s["prev_units"][0])
                act.wait_ge(ntopped, g * HEADS + hd + 1)
                for k in (0, 1):
                    act.activation(prob[:, k, 0:P], psS[k][:, 0:P], ACT.Exp, scale=SCALE,
                                   bias=ntop[:, k, 0:1], accum_out=ssum[:, k, 0:1])
                    act.activation(prob[:, k, P:3 * P], psS[k][:, 2 * P:4 * P], ACT.Exp, scale=SCALE,
                                   bias=ntop[:, k, 1:2], accum_out=ssum[:, k, 1:2]).then_inc(exped, 1)
                if s["next_qk"]:
                    project_hi(qk_hi[:, par, 0], proj_base(g) + s["q"], proj_bank(s["q"]))
                if s["prev"]:
                    transposed_copy(g, s["prev_units"][1])
                if s["next_qk"]:
                    project_hi(qk_hi[:, par, 1], proj_base(g) + s["k"], proj_bank(s["k"]))
                for f in extra.get((s["p"], s["h"], "a"), ()):
                    f()

                def z():
                    if s["prev"]:
                        z_high(s["prev_h"], zo_base(g) + s["z"], zo_bank(s["z"]))

                if s["h"] == 0:
                    z()
                for t, i in s["v"]:
                    project_hi(v_hi[:, 1 - s["p"], t], proj_base(g) + i, proj_bank(i))
                if s["h"]:
                    z()
                for f in extra.get((s["p"], s["h"], "c"), ()):
                    f()

        def extras(g, plan):
            first = isinstance(g, int) and g == 0
            c2 = cond_act(act, g, 1)
            out = {
                (1, 0, "a"): [lambda: refill("v", g + 1, freed=(projected, proj_base(g) + last_event(plan, 0, "v") + 1))],
                (1, 0, "c"): [lambda: refill("qk", g + 1, 0, (projected, proj_base(g) + plan[3]["k"] + 1))],
                (1, 1, "a"): [lambda: refill("qk", g + 1, 1, (projected, proj_base(g) + plan[4]["k"] + 1))],
                (1, 2, "a"): [lambda: refill("qk", g + 1, 2, (projected, proj_base(g) + plan[5]["k"] + 1))],
                (1, 3, "a"): [lambda: refill("qk", g + 1, 3, (projected, proj_base(g) + plan[6]["k"] + 1))],
            }
            if first:
                out[(0, 0, "a")] = [lambda: next(c[2]), lambda: next(c[3])]
                out[(0, 0, "c")] = [lambda: next(c[2])]
                out[(0, 1, "a")] = [lambda: next(c[3])]
                out[(0, 1, "c")] = [lambda: next(c[2])]
                out[(0, 2, "c")] = [lambda: next(c[3])]
                out[(1, 1, "c")] = [lambda: next(c2)]
            else:
                out[(0, 0, "c")] = [lambda: next(c2)]
                out[(0, 2, "a")] = [lambda: refill("o", g, freed=(zo_done, zo_base(g) + MIDDLE[1]["o"][-1][1] + 1))]
            if plan is LAST:
                out[(1, 1, "c")] = [lambda: y2_exp(0), lambda: y2_exp(1)]
                out[(1, 3, "c")] = [lambda: y2_hi(0), lambda: y2_hi(1)]
            return out

        def y2_exp(b):
            act.wait_ge(zo_read, ZO_X0 if b < 2 else ZO_TOTAL + CB)
            act.wait_ge(c2_dve, B * COND2_DVE)
            act.activation(y2_tile(b), cols(xT, b), ACT.Exp, scale=-1.0).then_inc(e_exp, 1)

        def y2_hi(b):
            act.wait_ge(y2f_done, b + 1)
            act.wait_ge(projected, proj_base(GROUPS - 1) + LAST[2]["k"] + 1 if b < 2 else PROJ_TOTAL)
            act.activation(cols(y_hi, b), y2_full(b), ACT.Copy).then_inc(y2hi_done, 1)

        group(0, FIRST, extras(0, FIRST))
        with act.Fori(1, GROUPS - 1) as g:
            group(g, MIDDLE, extras(g, MIDDLE))
        group(GROUPS - 1, LAST, extras(GROUPS - 1, LAST))
        for k in (-2, -1):
            transposed_copy(GROUPS, k)
        z_high(GH - 1, ZO_UNITS, zo_bank(ZO_GROUP))

        def gate_exp(p):
            act.wait_ge(gate_step, p * GATE_STEPS + 2 + 2 * TB)
            act.activation(gw2[:], gap[:], ACT.Exp).then_inc(gap_exp, 1)

        def copies(p):
            act.wait_ge(gT_done, p + 1)
            act.activation(gatesT[:, p], psS[1][0:E, :], ACT.Copy).then_inc(gT_copied, 1)
            for k in range(2):
                act.wait_ge(based, 2 * p + k + 1)
                act.activation(acc[:, p * TB + 2 * k:p * TB + 2 * k + 2],
                               psA[k][:].rearrange("p (a n) -> p a n", a=2), ACT.Copy).then_inc(base_copied, 1)

        gate_exp(0)
        refill("o", GROUPS, freed=(zo_done, ZO_TOTAL + CB))
        for b in range(2, 4):
            y2_exp(b)
        copies(0)
        for b in range(2, 4):
            y2_hi(b)
        gate_exp(1)
        copies(1)

    @block.vector
    def _(dve):
        dve.wait_ge(in_small, 32)
        dve.tensor_reduce(tsum[:], temb[:], AX.X, ALU.add).then_inc(pre_dve, 1)
        dve.wait_ge(pre_act, 3)
        dve.tensor_scalar(tf[:], tf[:], 1.0, None, ALU.add).then_inc(pre_dve, 1)
        dve.wait_ge(pre_dve, 2)
        dve.reciprocal(tf[:], tf[:]).then_inc(pre_dve, 1)
        dve.wait_ge(pre_dve, 3)
        dve.tensor_scalar(tdec[:], tf[:], 0.5, 0.5, ALU.mult, ALU.add).then_inc(pre_dve, 1)
        dve.tensor_scalar(tout[:], tf[:], 0.2, 0.8, ALU.mult, ALU.add).then_inc(pre_dve, 1)
        dve.wait_ge(pre_dve, 5)
        for w in range(2):
            for c in range(CB):
                dve.tensor_scalar(decay[:, w, c], tdec[:], ew[:, w, c:c + 1], None, ALU.mult).then_inc(pre_dve, 1)
        dve.memset(pT[:, :, :, 0:P].bitcast(F32), 0.0).then_inc(pre_dve, 1)
        dve.wait_ge(pre_dve, 10)

        def project_lo(out, hi, i, bank):
            dve.wait_ge(proj_hi, i + 1)
            dve.tensor_tensor(out, psA[bank][:], hi.bitcast(F32), ALU.subtract).then_inc(proj_lo, 1)

        c = [cond_dve(dve, b, 0) for b in range(B)]
        for b in (0, 1, 0, 1, 0, 0, 0, 1, 0, 1, 1, 1):
            next(c[b])
        for t in range(TB):
            project_lo(v_lo[:, 0, t], v_hi[:, 0, t], t, proj_bank(t))
        for j in range(2):
            project_lo(qk_lo[:, 0, j], qk_hi[:, 0, j], TB + j, proj_bank(TB + j))

        def maxima(g, hd):
            for k in (0, 1):
                dve.wait_ge(scored, g * UNITS_GROUP + 2 * hd + k + 1)
                dve.tensor_reduce(top[:, k, 0:1], psS[k][:, 0:P], AX.X, ALU.max).then_inc(topped, 1)
                dve.tensor_reduce(top[:, k, 1:2], psS[k][:, 2 * P:4 * P], AX.X, ALU.max).then_inc(topped, 1)
            dve.wait_ge(topped, 4 * (g * HEADS + hd + 1))
            dve.tensor_scalar(ntop[:], top[:], -SCALE, None, ALU.mult).then_inc(ntopped, 1)

        def sums(g, hd):
            dve.wait_ge(exped, 2 * (g * HEADS + hd + 1))
            dve.tensor_scalar(ssmall[:], ssum[:], 1.0 / LIFT, None, ALU.mult).then_inc(summed, 1)

        def reciprocals(g, hd):
            dve.wait_ge(summed, g * HEADS + hd + 1)
            dve.reciprocal(rsum[:], ssmall[:]).then_inc(recipd, 1)

        ROWS = ((slice(0, P), 0), (slice(P, 3 * P), 1))

        def high_part(g, hd, k):
            if k == 0:
                dve.wait_ge(recipd, g * HEADS + hd + 1)
            if not (isinstance(g, int) and g == 0 and hd == 0):
                dve.wait_ge(transposed, g * UNITS_GROUP + 2 * hd + k - 1)
            for c, q in ROWS:
                dve.tensor_scalar(prob16[:, k, 0, c], prob[:, k, c], rsum[:, k, q:q + 1], None, ALU.mult).then_inc(halved_hi, 1)

        def low_part(g, hd, k):
            dve.wait_ge(halved_hi, 2 * (g * UNITS_GROUP + 2 * hd + k) + 2)
            for c, q in ROWS:
                dve.scalar_tensor_tensor(prob16[:, k, 1, c], prob[:, k, c], rsum[:, k, q:q + 1], prob16[:, k, 0, c],
                                         ALU.mult, ALU.subtract).then_inc(halved, 1)

        def add_output(p, c, i, bank):
            dve.wait_ge(zo_done, i + 1)
            dve.wait_ge(zo_read, i)
            x = xT[:, c, p * PAIR:(p + 1) * PAIR]
            dve.tensor_tensor(x, psZ[bank][:], x, ALU.add).then_inc(zo_read, 1)

        def z_low(h, n, bank):
            dve.wait_ge(z_hi_done, n)
            dve.scalar_tensor_tensor(z_lo[:, h], psZ[bank][:], 1.0 / LIFT, z_hi[:, h].bitcast(F32),
                                     ALU.mult, ALU.subtract).then_inc(zo_read, 1)

        def group(g, plan, extra):
            for s in plan:
                hd, par = s["hd"], (s["hd"] + 1) % 2
                maxima(g, hd)
                if hd > 1:
                    z_low((hd - 2) % GH, g * HEADS + hd - 1, zo_bank(plan[hd - 1]["z"]))
                elif not (isinstance(g, int) and g == 0):
                    z_low((hd - 2) % GH, g * HEADS + hd - 1, zo_bank(plan[hd - 1]["z"] if hd else -1))
                if s["next_qk"]:
                    project_lo(qk_lo[:, par, 0], qk_hi[:, par, 0], proj_base(g) + s["q"], proj_bank(s["q"]))
                sums(g, hd)
                if s["next_qk"]:
                    project_lo(qk_lo[:, par, 1], qk_hi[:, par, 1], proj_base(g) + s["k"], proj_bank(s["k"]))
                reciprocals(g, hd)
                high_part(g, hd, 0)
                high_part(g, hd, 1)
                low_part(g, hd, 0)
                low_part(g, hd, 1)
                for c, i in s["o"]:
                    add_output(1 - s["p"], c, zo_base(g) + i, zo_bank(i))
                for f in extra.get((s["p"], s["h"], "a"), ()):
                    f()
                for t, i in s["v"]:
                    project_lo(v_lo[:, 1 - s["p"], t], v_hi[:, 1 - s["p"], t], proj_base(g) + i, proj_bank(i))
                for f in extra.get((s["p"], s["h"], "c"), ()):
                    f()

        def extras(g, plan):
            c2 = cond_dve(dve, g, 1)
            n2 = lambda: next(c2)
            if isinstance(g, int) and g == 0:
                n0, n1 = lambda: next(c[2]), lambda: next(c[3])
                out = {(0, 0, "a"): [n0, n1], (0, 0, "c"): [n0, n0, n0], (0, 1, "a"): [n1, n0], (0, 1, "c"): [n0, n1],
                       (0, 2, "a"): [n1, n1], (0, 2, "c"): [n1],
                       (1, 1, "a"): [n2], (1, 1, "c"): [n2], (1, 2, "a"): [n2], (1, 2, "c"): [n2], (1, 3, "c"): [n2]}
            else:
                out = {(0, 0, "a"): [n2], (0, 1, "a"): [n2], (0, 1, "c"): [n2], (0, 2, "c"): [n2], (0, 3, "c"): [n2]}
            if plan is LAST:
                out[(1, 2, "a")] = [lambda: y2_first(0)]
                out[(1, 2, "c")] = [lambda: y2_second(0), lambda: y2_first(1)]
                out[(1, 3, "a")] = [lambda: y2_second(1)]
                out[(1, 3, "c")] = [lambda: y2_lo(0), lambda: y2_lo(1)]
            return out

        def y2_first(b):
            dve.wait_ge(e_exp, b + 1)
            dve.scalar_tensor_tensor(y2_tile(b), y2_tile(b), 1.0, cols(den2, b), ALU.add, ALU.mult).then_inc(e_dve, 1)
            dve.wait_ge(e_dve, 2 * b + 1)
            dve.reciprocal(y2_tile(b), y2_tile(b)).then_inc(e_dve, 1)

        def y2_second(b):
            dve.wait_ge(e_dve, 2 * b + 2)
            dve.tensor_tensor(y2_full(b), y2_tile(b), cols(num2, b), ALU.mult).then_inc(y2f_done, 1)

        def y2_lo(b):
            dve.wait_ge(y2hi_done, b + 1)
            dve.tensor_tensor(cols(y_lo, b), y2_full(b), cols(y_hi, b).bitcast(F32), ALU.subtract).then_inc(y2lo_done, 1)

        group(0, FIRST, extras(0, FIRST))
        with dve.Fori(1, GROUPS - 1) as g:
            group(g, MIDDLE, extras(g, MIDDLE))
        group(GROUPS - 1, LAST, extras(GROUPS - 1, LAST))
        z_low(GH - 2, GROUPS * HEADS - 1, zo_bank(-1))
        z_low(GH - 1, GROUPS * HEADS, zo_bank(ZO_GROUP))

        def gate(p):
            n = [p * GATE_STEPS]

            def step(ins):
                n[0] += 1
                ins.then_inc(gate_step, 1)

            dve.wait_ge(logits_done, p + 1)
            if p:
                dve.wait_ge(gates_done, p)
            step(dve.tensor_copy(logit[:].rearrange("p t e -> p (t e)"), psS[0][:, p * 256:p * 256 + TB * E]))
            dve.wait_ge(gate_step, n[0])
            for t in range(TB):
                step(dve.max(best[:, t], logit[:, t]))
            dve.wait_ge(gate_step, n[0])
            for t in range(TB):
                step(dve.max_index(besti[:, t], best[:, t], logit[:, t]))
            step(dve.tensor_tensor(gap[:], best[:, :, 1], best[:, :, 0], ALU.subtract))
            dve.wait_ge(gate_step, n[0])
            step(dve.tensor_copy(bestf[:], besti[:]))
            dve.wait_ge(gap_exp, p + 1)
            step(dve.tensor_scalar(gden[:], gw2[:], 1.0, None, ALU.add))
            dve.wait_ge(gate_step, n[0])
            step(dve.reciprocal(gw1[:], gden[:]))
            dve.wait_ge(gate_step, n[0])
            step(dve.tensor_tensor(gw2[:], gw2[:], gw1[:], ALU.mult))
            dve.wait_ge(gate_step, n[0])
            for t in range(TB):
                step(dve.tensor_scalar(gates[:, p, t], iota[:], bestf[:, t, 0:1], gw1[:, t:t + 1], ALU.is_equal, ALU.mult))
                step(dve.tensor_scalar(gsec[:, t], iota[:], bestf[:, t, 1:2], gw2[:, t:t + 1], ALU.is_equal, ALU.mult))
            dve.wait_ge(gate_step, n[0])
            dve.tensor_tensor(gates[:, p], gates[:, p], gsec[:], ALU.add).then_inc(gates_done, 1)

        def add_experts(j):
            p, slot, t = j // (4 * TB), j // TB % 4, j % TB
            a = acc[:, p * TB + t]
            dve.wait_ge(base_copied, 2 * p + t // 2 + 1)
            dve.wait_ge(expert_done, j + 1)
            if slot:
                dve.wait_ge(expert_read, j - TB + 1)
            for e in range(2):
                if e:
                    dve.wait_ge(expert_half, j + 1)
                ins = dve.scalar_tensor_tensor(a, psE[j % 4][:, e * C:(e + 1) * C], gates[:, p, t, 2 * slot + e:2 * slot + e + 1],
                                               a, ALU.mult, ALU.add)
                ins.then_inc(expert_read if e else expert_half, 1)

        gate(0)
        for c in range(CB):
            add_output(1, c, ZO_TOTAL + c, zo_bank(ZO_GROUP + 1 + c))
        work = {2: [lambda: y2_first(2)], 5: [lambda: y2_second(2), lambda: y2_first(3)],
                8: [lambda: y2_second(3), lambda: y2_lo(2)], 9: [lambda: y2_lo(3)], 13: [lambda: gate(1)]}
        for j in range(8 * TB):
            add_experts(j)
            for f in work.get(j, ()):
                f()

    @block.tensor
    def _(pe):
        def three(out, pairs, start=True, stop=True):
            n = len(pairs)
            for k, ((ah, al), (bh, bl)) in enumerate(pairs):
                pe.matmul(out, ah, bh, start=start and k == 0, stop=False)
                pe.matmul(out, ah, bl, start=False, stop=False)
                ins = pe.matmul(out, al, bh, start=False, stop=stop and k == n - 1)
            return ins

        def both(hi, lo, *index):
            return hi[index], lo[index]

        def bank_free(i):
            if not (isinstance(i, int) and i < 3):
                pe.wait_ge(proj_lo, i - 2)

        def project_qk(j, h, p, i, bank):
            bank_free(i)
            three(psA[bank][:], [(both(w_hi, w_lo, slice(None), SLOT_Q + j, c, slice(h * DH, (h + 1) * DH)),
                                  both(y_hi, y_lo, slice(None), c, slice(p * PAIR, (p + 1) * PAIR)))
                                 for c in range(CB)]).then_inc(projected, 1)

        def project_v(t, p, i, bank):
            bank_free(i)
            k = p * PAIR + t * P
            three(psA[bank][:], [(both(y_hi, y_lo, slice(None), c, slice(k, k + P)),
                                  both(w_hi, w_lo, slice(None), SLOT_V, c)) for c in range(CB)]).then_inc(projected, 1)

        def scores(g, k, par):
            b = k % 2
            if not (isinstance(g, int) and g * UNITS_GROUP + k < 2):
                pe.wait_ge(exped, g * UNITS_GROUP + k - 1)
            for q in range(2):
                out, tokens = psS[b][:, q * T:(q + 1) * T], slice(b * T + q * P, b * T + q * P + P)
                keys_hi, keys_lo = (t[:, par, 1, b * T:(b + 1) * T] for t in (qk_hi, qk_lo))
                pe.matmul(out, qk_hi[:, par, 0, tokens], keys_hi, start=True, stop=False)
                pe.matmul(out, qk_hi[:, par, 0, tokens], keys_lo, start=False, stop=False)
                pe.matmul(out[:, q * P:(q + 1) * P], identb[:], negmask[:], start=False, stop=False)
                ins = pe.matmul(out, qk_lo[:, par, 0, tokens], keys_hi, start=False, stop=True)
            ins.then_inc(scored, 1)

        def transposes(g, k):
            u = k % 2
            pe.wait_ge(halved, 2 * (g * UNITS_GROUP + k + 1))
            if not (isinstance(g, int) and g * UNITS_GROUP + k < 1):
                pe.wait_ge(pT_ready, g * UNITS_GROUP + k)
            for part in range(2):
                for n, c in enumerate((2, 0, 1)):
                    o = (part * 3 + n) * P
                    ins = pe.transpose(psT[:, o:o + P], prob16[:, u, part, c * P:(c + 1) * P], ident16[:])
            ins.then_inc(transposed, 1)

        def zo_free(i):
            if not (isinstance(i, int) and i < 2):
                pe.wait_ge(zo_read, i - 1)

        def values(n, h, p, i, bank):
            zo_free(i)
            for b in range(2):
                pe.wait_ge(pT_ready, n + b + 1)
                ins = three(psZ[bank][:, b * T:(b + 1) * T],
                            [(both(v_hi, v_lo, slice(None), p, 2 * b + kb, slice(h * DH, (h + 1) * DH)),
                              (pT[:, b, 0, (1 - kb) * T:(2 - kb) * T], pT[:, b, 1, (1 - kb) * T:(2 - kb) * T]))
                             for kb in range(2)])
            ins.then_inc(zo_done, 1)

        def output(c, i, bank):
            zo_free(i)
            pe.wait_ge(zo_read, i - c)
            three(psZ[bank][:], [(both(w_o_hi, w_o_lo, slice(None), h, slice(c * P, (c + 1) * P)),
                                  both(z_hi, z_lo, slice(None), h)) for h in range(GH)]).then_inc(zo_done, 1)

        w_o_hi = w_hi[:, SLOT_O].rearrange("p c n -> p (c n)").rearrange("p (h n) -> p h n", h=GH)
        w_o_lo = w_lo[:, SLOT_O].rearrange("p c n -> p (c n)").rearrange("p (h n) -> p h n", h=GH)

        pe.wait_ge(yhi_done, 2)
        pe.wait_ge(ylo_done, 2)
        pe.wait_ge(wlo_v, 1)
        for t in range(TB):
            project_v(t, 0, t, proj_bank(t))
        pe.wait_ge(wlo_qk, 1)
        for j in range(2):
            project_qk(j, 0, 0, TB + j, proj_bank(TB + j))
        pe.wait_ge(consts, 4 + E)
        pe.wait_ge(pre_dve, 10)

        def group(g, plan):
            for s in plan:
                p, h, par = s["p"], s["h"], s["hd"] % 2
                units = [2 * s["hd"], 2 * s["hd"] + 1]
                if s["hd"]:
                    pe.wait_ge(proj_lo, proj_base(g) + plan[s["hd"] - 1]["k"] + 1)
                elif isinstance(g, int) and g == 0:
                    pe.wait_ge(proj_lo, PROJ_AHEAD)
                else:
                    pe.wait_ge(proj_lo, proj_base(g) - PROJ_GROUP + MIDDLE[-1]["k"] + 1)
                for k in units:
                    scores(g, k, par)
                if s["prev"]:
                    transposes(g, s["prev_units"][0])
                nh, np_ = (h + 1) % GH, (p if h < GH - 1 else 1 - p)
                ng = g if s["hd"] < HEADS - 1 else g + 1
                if s["next_qk"]:
                    pe.wait_ge(wlo_qk, ng * GH + nh + 1)
                    if isinstance(g, int) and g == 0 and p == 0 and h == GH - 1:
                        pe.wait_ge(yhi_done, 4)
                        pe.wait_ge(ylo_done, 4)
                    project_qk(0, nh, np_, proj_base(g) + s["q"], proj_bank(s["q"]))
                if s["prev"]:
                    transposes(g, s["prev_units"][1])
                if s["next_qk"]:
                    project_qk(1, nh, np_, proj_base(g) + s["k"], proj_bank(s["k"]))
                for c, i in s["o"]:
                    pe.wait_ge(wlo_o, g + (1 if p == 1 else 0))
                    output(c, zo_base(g) + i, zo_bank(i))

                def z():
                    if s["prev"]:
                        values(g * UNITS_GROUP + s["prev_units"][0], s["prev_h"], s["prev_p"],
                               zo_base(g) + s["z"], zo_bank(s["z"]))

                if h == 0:
                    z()
                for t, i in s["v"]:
                    if isinstance(g, int) and g == 0 and p == 0:
                        pe.wait_ge(yhi_done, 3 + t // 2)
                        pe.wait_ge(ylo_done, 3 + t // 2)
                    pe.wait_ge(wlo_v, g + 1 + p)
                    project_v(t, 1 - p, proj_base(g) + i, proj_bank(i))
                if h:
                    z()

        group(0, FIRST)
        with pe.Fori(1, GROUPS - 1) as g:
            group(g, MIDDLE)
        group(GROUPS - 1, LAST)
        for k in (-2, -1):
            transposes(GROUPS, k)
        def logits(p):
            pe.wait_ge(y2f_done, 2 * p + 2)
            if p == 0:
                pe.wait_ge(exped, GROUPS * UNITS_GROUP)
            else:
                pe.wait_ge(gates_done, p)
            for t in range(TB):
                for c in range(CB):
                    k = (t % 2) * P
                    ins = pe.matmul(psS[0][:, p * 256 + t * E:p * 256 + (t + 1) * E], y2_full(2 * p + t // 2)[:, c, k:k + P],
                                    gate_w[:, c], start=c == 0, stop=c == CB - 1)
            ins.then_inc(logits_done, 1)

        def last_head():
            values(GROUPS * UNITS_GROUP - 2, GH - 1, NPAIR - 1, ZO_UNITS, zo_bank(ZO_GROUP))
            pe.wait_ge(wlo_o, GROUPS)
            for c in range(CB):
                output(c, ZO_TOTAL + c, zo_bank(ZO_GROUP + 1 + c))

        def gates_turn(p):
            pe.wait_ge(gates_done, p + 1)
            if p:
                pe.wait_ge(gT_copied, p)
            for t in range(TB):
                ins = pe.transpose(psS[1][0:E, t * P:(t + 1) * P], gates[:, p, t], identf[:])
            ins.then_inc(gT_done, 1)

        def base(p):
            pe.wait_ge(gT_copied, p + 1)
            if p:
                pe.wait_ge(base_copied, 2 * p)
            for k in range(2):
                for tt in range(2):
                    t = 2 * k + tt
                    n = p * PAIR + t * P
                    for c in range(CB):
                        o = psA[k][:, tt * C + c * P:tt * C + (c + 1) * P]
                        pe.matmul(o, gatesT[:, p, t * P:(t + 1) * P], expert_b[:, c * P:(c + 1) * P], start=True, stop=False)
                        ins = pe.matmul(o, xT[:, c, n:n + P], identf[:], start=False, stop=True)
                ins.then_inc(based, 1)

        def experts(j):
            p, slot, t = j // (4 * TB), j // TB % 4, j % TB
            if j >= 4:
                pe.wait_ge(expert_read, j - 3)
            elif j < 2:
                pe.wait_ge(zo_read, ZO_TOTAL + j + 1)
            elif j == 2:
                pe.wait_ge(pT_ready, GROUPS * UNITS_GROUP)
            else:
                pe.wait_ge(proj_lo, PROJ_TOTAL)
            if j < 4 * TB:
                if slot == 0:
                    pe.wait_ge(wlo_v, GROUPS + 1)
                elif slot < 3:
                    pe.wait_ge(wlo_qk, (GROUPS + 1) * GH)
                else:
                    pe.wait_ge(wlo_o, GROUPS + 1)
            pe.wait_ge(y2lo_done, 2 * p + t // 2 + 1)
            n = p * PAIR + t * P
            three(psE[j % 4], [(both(y_hi, y_lo, slice(None), c, slice(n, n + P)),
                                both(w_hi, w_lo, slice(None), EXPERT_SLOTS[slot], c)) for c in range(CB)]).then_inc(expert_done, 1)

        pe.wait_ge(in_late, 32)
        logits(0)
        last_head()
        experts(0)
        gates_turn(0)
        experts(1)
        base(0)
        for j in range(2, 8 * TB):
            experts(j)
            if j == 12:
                logits(1)
            if j == 4 * TB + 1:
                gates_turn(1)
            if j == 4 * TB + 2:
                base(1)
    return None


def lay_out(inputs):
    import numpy as np

    def channels_first(a):
        return np.ascontiguousarray(a.reshape(N, CB, P).transpose(2, 1, 0))

    def by_channel(a):
        return a.reshape(a.shape[0], CB, P).transpose(2, 1, 0)

    weights = np.empty((GROUPS + 1, P, 4, CB, GH * DH), np.float32)
    for slot, name in ((SLOT_Q, "L0_attn_W_Q"), (SLOT_K, "L0_attn_W_K"), (SLOT_V, "L0_attn_W_V")):
        w = inputs[name]
        for g in range(GROUPS):
            weights[g, :, slot] = by_channel(w[g * GH:(g + 1) * GH].reshape(GH * DH, C))
    wo = inputs["L0_attn_W_O"].reshape(C, GROUPS, GH, DH).transpose(1, 3, 2, 0)
    weights[:GROUPS, :, SLOT_O] = wo.reshape(GROUPS, P, CB, GH * DH)
    we = inputs["L0_ffn_expert_w"].reshape(4, 2, CB, P, C).transpose(0, 3, 2, 1, 4)
    for k, slot in enumerate(EXPERT_SLOTS):
        weights[GROUPS, :, slot] = we[k].reshape(P, CB, GH * DH)
    wu = np.stack([inputs[n].reshape(CB, P).T for n in ("L0_cond_w", "L0_cond_u", "L0_cond2_w", "L0_cond2_u")], 1)
    return {
        "xT": channels_first(inputs["x"]),
        "fT": channels_first(inputs["fside_BxSxS_0"]),
        "temb": np.ascontiguousarray(inputs["cond_512"]),
        "wu": np.ascontiguousarray(wu),
        "weights": weights,
        "gate_w": np.ascontiguousarray(by_channel(inputs["L0_ffn_gate_w"])),
        "expert_b": np.ascontiguousarray(inputs["L0_ffn_expert_b"]),
    }


def kernel(**inputs):
    from contextlib import ExitStack
    import numpy as np
    import concourse.bacc as bacc
    from concourse.bass_utils import run_bass_kernel_spmd

    arrays = lay_out({k: np.asarray(v) for k, v in inputs.items()})
    nc = bacc.Bacc("TRN2", target_bir_lowering=False, num_devices=1)
    aps = {n: nc.dram_tensor("in_" + n, a.shape, F32, kind="ExternalInput").ap() for n, a in arrays.items()}
    aps["out"] = nc.dram_tensor("out", (N, C), F32, kind="ExternalOutput").ap()
    with ExitStack() as ctx:
        build(nc, ctx, aps)
    r = run_bass_kernel_spmd(nc, [{"in_" + n: a for n, a in arrays.items()}], core_ids=[0])
    return r.results[0]["out"].reshape(B, T, C)
```

```python
import concourse.bass as bass
import concourse.mybir as mybir
from concourse.alu_op_type import AluOpType as ALU

ACT = mybir.ActivationFunctionType
AX = mybir.AxisListType
F32, F32R, F16 = mybir.dt.float32, mybir.dt.float32r, mybir.dt.float16
BF16, U32 = mybir.dt.bfloat16, mybir.dt.uint32

P = 128
B, T, C = 4, 256, 256
TD = 64
H, DH = 16, 128
E = 8
CB = C // P
N = B * T
PAIR = 2 * T
NPAIR = B // 2
GROUPS, GH = 4, 4
HEADS = NPAIR * GH
TB = PAIR // P
SLOT = CB * GH * DH
SLOT_Q, SLOT_K, SLOT_V, SLOT_O = range(4)
EXPERT_SLOTS = (SLOT_V, SLOT_Q, SLOT_K, SLOT_O)
SCALE = float(DH) ** -0.5
MASKED = -1e10
LIFT = 2.0 ** 15

PROJ_AHEAD = TB + 2
PROJ_GROUP = HEADS * 2 + NPAIR * TB
UNITS_GROUP = HEADS * 2
ZO_GROUP = HEADS + NPAIR * CB
SUMS = ("vector", "tensor", "gpsimd", "gpsimd")
COND1_DVE, COND1_ACT, COND1_POOL = (17, 15, 15, 15), 4, (5, 3, 7, 7)
GATE_STEPS = 3 + 4 * TB
COND2_DVE, COND2_ACT, COND2_POOL = 15, 3, 7


def head_plan(group):
    proj, zo = 0, (1 + CB if group == "first" else 0)
    steps = []
    for p in range(NPAIR):
        for h in range(GH):
            last_pair = group == "last" and p == NPAIR - 1
            step = {"p": p, "h": h, "hd": p * GH + h}
            step["next_qk"] = not (last_pair and h == GH - 1)
            if step["next_qk"]:
                step["q"] = proj
                proj += 1
                step["k"] = proj
                proj += 1
            step["v"] = []
            early = p == 0 and group != "first"
            chunks = [[0], [], [1], [2, 3]] if early else [[], [], [0, 1], [2, 3]]
            if not last_pair:
                for t in chunks[h]:
                    step["v"].append((t, proj))
                    proj += 1
            step["o"] = []
            if h == 1 and not (group == "first" and p == 0):
                for c in range(CB):
                    step["o"].append((c, zo))
                    zo += 1
            step["prev"] = not (group == "first" and p == 0 and h == 0)
            step["prev_h"], step["prev_p"] = (h - 1) % GH, p if h else 1 - p
            step["prev_units"] = [2 * step["hd"] - 2, 2 * step["hd"] - 1] if step["prev"] else []
            step["z"] = zo
            zo += step["prev"]
            steps.append(step)
    return steps


FIRST, MIDDLE, LAST = head_plan("first"), head_plan("middle"), head_plan("last")
PROJ_TOTAL = PROJ_AHEAD + PROJ_GROUP * (GROUPS - 1) + max(s["k"] for s in LAST if s["next_qk"]) + 1


def zo_base(g):
    return ZO_GROUP * g - 1 - CB


ZO_UNITS = zo_base(GROUPS)
ZO_TOTAL = ZO_UNITS + 1
ZO_X0 = zo_base(GROUPS - 1) + LAST[GH + 1]["o"][-1][1] + 1


def proj_base(g):
    return PROJ_GROUP * g + PROJ_AHEAD


def proj_bank(i):
    return i % 3


def zo_bank(i):
    return (i + zo_base(0)) % 2


def last_event(plan, p, kind):
    return max(e for s in plan if s["p"] == p for _, e in s[kind])


def build(nc, ctx, ap):
    def sb(name, shape, dt):
        return ctx.enter_context(nc.sbuf_tensor(name, shape, dt))

    def sem(name):
        return ctx.enter_context(nc.semaphore(name))

    xT = sb("xT", [P, CB, N], F32)
    fT = sb("fT", [P, CB, N], F32)
    wu = sb("wu", [P, 4, CB], F32)
    temb = sb("temb", [P, B, TD], F32)
    gate_w = sb("gate_w", [P, CB, E], F32)
    expert_b = sb("expert_b", [E, C], F32)
    identf = sb("identf", [P, P], F32)
    ident16 = sb("ident16", [P, P], F16)
    identb = sb("identb", [P, P], BF16)
    negmask = sb("negmask", [P, P], BF16)
    iota = sb("iota", [P, E], F32)
    tsum = sb("tsum", [P, B], F32)
    tf = sb("tf", [P, B], F32)
    tdec = sb("tdec", [P, B], F32)
    tout = sb("tout", [P, B], F32)
    ew = sb("ew", [P, 2, CB], F32)
    decay = sb("decay", [P, 2, CB, B], F32)
    tiles = sb("tiles", [P, 2, 7, CB, T], F32)
    ratio2 = sb("ratio2", [P, CB, N], F32)
    y2 = sb("y2", [P, CB, N], F32)
    y_hi = sb("y_hi", [P, CB, N], F32R)
    y_lo = sb("y_lo", [P, CB, N], F32R)
    raw = sb("raw", [P, 4, CB, GH * DH], F32)
    w_hi = sb("w_hi", [P, 4, CB, GH * DH], F32R)
    w_lo = sb("w_lo", [P, 4, CB, GH * DH], F32R)
    qk_hi = sb("qk_hi", [P, 2, 2, PAIR], F32R)
    qk_lo = sb("qk_lo", [P, 2, 2, PAIR], F32R)
    v_hi = sb("v_hi", [P, NPAIR, TB, GH * DH], F32R)
    v_lo = sb("v_lo", [P, NPAIR, TB, GH * DH], F32R)
    top = sb("top", [P, 2, 2], F32)
    ntop = sb("ntop", [P, 2, 2], F32)
    ssum = sb("ssum", [P, 2, 2], F32)
    ssmall = sb("ssmall", [P, 2, 2], F32)
    rsum = sb("rsum", [P, 2, 2], F32)
    prob = sb("prob", [P, 2, 3 * P], F32)
    prob16 = sb("prob16", [P, 2, 2, 3 * P], F16)
    pT = sb("pT", [P, 2, 2, 4 * P], F32R)
    z_hi = sb("z_hi", [P, GH, PAIR], F32R)
    z_lo = sb("z_lo", [P, GH, PAIR], F32R)
    logit = sb("logit", [P, TB, E], F32)
    best = sb("best", [P, TB, E], F32)
    besti = sb("besti", [P, TB, E], U32)
    bestf = sb("bestf", [P, TB, E], F32)
    gap = sb("gap", [P, TB], F32)
    gw2 = sb("gw2", [P, TB], F32)
    gw1 = sb("gw1", [P, TB], F32)
    gsec = sb("gsec", [P, TB, E], F32)
    gates = sb("gates", [P, NPAIR, TB, E], F32)
    gatesT = tiles[0:E, 0, 2:2 + NPAIR].rearrange("e p c n -> e p (c n)")
    acc = fT[:, :, :].rearrange("p c (k o) -> p (c k) o", o=C)

    def ps(name, dt=F32):
        return ctx.enter_context(nc.psum_tensor(name, [P, 512 if dt == F32 else 1024], dt))

    psA = [ps("psA0"), ps("psA1"), ps("psA2")]
    psS = [ps("psS0"), ps("psS1")]
    psT = ps("psT", F16)
    psZ = [ps("psZ0"), ps("psZ1")]
    psSum = psS
    psE = [psA[0], psA[1], psZ[0], psZ[1]]
    psG = psA[2]
    psB = psS

    in_small, in_f0, in_x0, in_f1, in_x1, in_late = (sem(f"in_{n}") for n in ("small", "f0", "x0", "f1", "x1", "late"))
    raw_v, raw_qk, raw_o = sem("raw_v"), sem("raw_qk"), sem("raw_o")
    consts = sem("consts")
    const_step = sem("const_step")
    pre_dve, pre_act = sem("pre_dve"), sem("pre_act")
    c1_dve, c1_act, c1_pool = ([sem(f"c1_{n}{k}") for k in range(2)] for n in ("dve", "act", "pool"))
    summed_pe = sem("summed_pe")
    c2_dve, c2_act, c2_pool = sem("c2_dve"), sem("c2_act"), sem("c2_pool")
    yhi_done, ylo_done = sem("yhi_done"), sem("ylo_done")
    whi_v, whi_qk, whi_o = sem("whi_v"), sem("whi_qk"), sem("whi_o")
    wlo_v, wlo_qk, wlo_o = sem("wlo_v"), sem("wlo_qk"), sem("wlo_o")
    projected, proj_hi, proj_lo = sem("projected"), sem("proj_hi"), sem("proj_lo")
    scored, topped, ntopped, exped = sem("scored"), sem("topped"), sem("ntopped"), sem("exped")
    summed, recipd, halved_hi, halved = sem("summed"), sem("recipd"), sem("halved_hi"), sem("halved")
    transposed, pT_ready = sem("transposed"), sem("pT_ready")
    zo_done, z_hi_done, zo_read = sem("zo_done"), sem("z_hi_done"), sem("zo_read")
    sigmoid2, y2_done, y2hi_done, y2lo_done = (sem(n) for n in ("sigmoid2", "y2_done", "y2hi_done", "y2lo_done"))
    logits_done, gate_step, gate_soft, gates_done = (sem(n) for n in ("logits_done", "gate_step", "gate_soft", "gates_done"))
    gT_done, gT_copied, based, base_copied = (sem(n) for n in ("gT_done", "gT_copied", "based", "base_copied"))
    expert_done, expert_half, expert_read, stored = (sem(n) for n in ("expert_done", "expert_half", "expert_read", "stored"))

    block = ctx.enter_context(nc.Block())

    @block.sync
    def _(sp):
        sp.dma_start(wu[:], ap["wu"]).then_inc(in_small, 16)
        sp.dma_start(temb[:], ap["temb"].partition_broadcast(P)).then_inc(in_small, 16)
        sp.dma_start(fT[:, :, 0:PAIR], ap["fT"][:, :, 0:PAIR]).then_inc(in_f0, 16)
        sp.dma_start(xT[:, :, 0:PAIR], ap["xT"][:, :, 0:PAIR]).then_inc(in_x0, 16)

        def load(g):
            if g:
                sp.wait_ge(wlo_v, g)
            sp.dma_start(raw[:, SLOT_V], ap["weights"][g, :, SLOT_V]).then_inc(raw_v, 16)
            if g:
                sp.wait_ge(wlo_qk, g * GH)
            sp.dma_start(raw[:, SLOT_Q:SLOT_K + 1], ap["weights"][g, :, SLOT_Q:SLOT_K + 1]).then_inc(raw_qk, 16)
            if g:
                sp.wait_ge(wlo_o, g)
            sp.dma_start(raw[:, SLOT_O], ap["weights"][g, :, SLOT_O]).then_inc(raw_o, 16)

        load(0)
        sp.dma_start(fT[:, :, PAIR:N], ap["fT"][:, :, PAIR:N]).then_inc(in_f1, 16)
        sp.dma_start(xT[:, :, PAIR:N], ap["xT"][:, :, PAIR:N]).then_inc(in_x1, 16)
        sp.dma_start(gate_w[:], ap["gate_w"]).then_inc(in_late, 16)
        sp.dma_start(expert_b[:], ap["expert_b"]).then_inc(in_late, 16)
        for g in range(1, GROUPS + 1):
            load(g)
        for k in range(NPAIR * TB):
            sp.wait_ge(expert_read, (k // TB) * 4 * TB + 3 * TB + k % TB + 1)
            sp.dma_start(ap["out"][k * P:(k + 1) * P, :], acc[:, k, :]).then_inc(stored, 16)
        sp.wait_ge(stored, 16 * NPAIR * TB)

    EK, EUK, EKV, DF, DB, NF, NB = range(7)
    VCOPY = tiles[:, 1, 6]

    spare = y2[:, :, 0:T]

    def keys(b):
        return fT[:, :, bass.ds(b * T, T)] if not isinstance(b, int) else fT[:, :, b * T:(b + 1) * T]

    def cols(t, b):
        return t[:, :, bass.ds(b * T, T)] if not isinstance(b, int) else t[:, :, b * T:(b + 1) * T]

    def col(t, b):
        return t[:, bass.ds(b, 1)] if not isinstance(b, int) else t[:, b:b + 1]

    def dec(w, c, b):
        d = decay[:, w, c]
        return (d[:, bass.ds(b, 1)] if not isinstance(b, int) else d[:, b:b + 1]).to_broadcast([P, T])

    def steps_of(b, w):
        if w == 0:
            k = b % 2
            n = b // 2
            return (lambda i: tiles[:, k, i]), (c1_dve[k], c1_act[k], c1_pool[k]), (n * COND1_DVE[k], n * COND1_ACT, n * COND1_POOL[k])
        return (lambda i: tiles[:, 0, i]), (c2_dve, c2_act, c2_pool), (b * COND2_DVE, b * COND2_ACT, b * COND2_POOL)

    def sums_on(b, w):
        return SUMS[b] if w == 0 else "gpsimd"

    def cond_dve(dve, b, w):
        tile, (done, act, pool), (d0, a0, p0) = steps_of(b, w)
        f = keys(b)
        if w == 0 and b >= 2:
            dve.wait_ge(done, d0)
            dve.wait_ge(act, a0)
            dve.wait_ge(pool, p0)
            dve.wait_ge(yhi_done, b - 1)
            dve.wait_ge(ylo_done, b - 1)
        if w == 1:
            dve.wait_ge(c1_dve[0], sum(COND1_DVE[0::2]))
            dve.wait_ge(c1_dve[1], sum(COND1_DVE[1::2]))
            dve.wait_ge(yhi_done, B)
            dve.wait_ge(ylo_done, B)
            if not isinstance(b, int) or b > 0:
                dve.wait_ge(done, d0)
                dve.wait_ge(pool, p0)
        if w == 0:
            dve.wait_ge(in_f0 if b < 2 else in_f1, 16)
        dve.tensor_scalar(tile(EK), f, 30.0, None, ALU.min).then_inc(done, 1)
        for c in range(CB):
            dve.tensor_scalar(tile(EUK)[:, c], f[:, c], wu[:, 2 * w + 1, c:c + 1], 30.0, ALU.add, ALU.min).then_inc(done, 1)
        yield
        dve.wait_ge(act, a0 + 1)
        for c in range(CB):
            dve.tensor_tensor_scan(tile(DF)[:, c], dec(w, c, b), tile(EK)[:, c], 0.0, ALU.mult, ALU.add).then_inc(done, 1)
        for c in range(CB):
            dve.tensor_tensor_scan(tile(DB)[:, c][:, ::-1], dec(w, c, b), tile(EK)[:, c][:, ::-1], 0.0, ALU.mult, ALU.add).then_inc(done, 1)
        yield
        dve.wait_ge(pool, p0 + 1)
        for c in range(CB):
            dve.tensor_tensor_scan(tile(NF)[:, c], dec(w, c, b), tile(EKV)[:, c], 0.0, ALU.mult, ALU.add).then_inc(done, 1)
        for c in range(CB):
            dve.tensor_tensor_scan(tile(NB)[:, c][:, ::-1], dec(w, c, b), tile(EKV)[:, c][:, ::-1], 0.0, ALU.mult, ALU.add).then_inc(done, 1)
        yield
        n = d0 + 11
        numerator, denominator = tile(NF), tile(DF)
        if sums_on(b, w) == "vector":
            dve.wait_ge(done, d0 + 7)
            dve.tensor_tensor(tile(DF), tile(DF), tile(DB), ALU.add).then_inc(done, 1)
            dve.wait_ge(pool, p0 + 2)
            dve.wait_ge(done, d0 + 12)
            dve.tensor_tensor(tile(DF), tile(DF), tile(EUK), ALU.add).then_inc(done, 1)
            yield
            n += 2
            dve.wait_ge(done, n)
        elif sums_on(b, w) == "gpsimd":
            dve.wait_ge(pool, p0 + 4)
        else:
            denominator, numerator = (bank[:].rearrange("p (c n) -> p c n", c=CB) for bank in psSum)
            dve.wait_ge(summed_pe, 1)
        if w == 0:
            dve.wait_ge(act, a0 + 4)
            dve.scalar_tensor_tensor(tile(DF), denominator, 1e-8, tile(EK), ALU.max, ALU.mult).then_inc(done, 1)
        else:
            dve.tensor_scalar(tile(DF), tile(DF), 1e-8, None, ALU.max).then_inc(done, 1)
        dve.wait_ge(done, n + 1)
        dve.reciprocal(tile(DB)[:, 0], tile(DF)[:, 0]).then_inc(done, 1)
        yield
        dve.reciprocal(tile(DB)[:, 1], tile(DF)[:, 1]).then_inc(done, 1)
        yield
        if sums_on(b, w) == "tensor":
            dve.wait_ge(summed_pe, 2)
        else:
            dve.wait_ge(pool, p0 + (7 if sums_on(b, w) == "gpsimd" else 5))
        dve.wait_ge(done, n + 3)
        y = tile(NB) if w == 0 else cols(ratio2, b)
        dve.scalar_tensor_tensor(y, numerator, col(tout, b), tile(DB), ALU.mult, ALU.mult).then_inc(done, 1)
        yield

    def cond_act(act, b, w):
        tile, (dve, done, pool), (d0, a0, p0) = steps_of(b, w)
        act.wait_ge(dve, d0 + 1)
        act.activation(tile(EK), tile(EK), ACT.Exp).then_inc(done, 1)
        if w == 1:
            act.activation(VCOPY, keys(b), ACT.Copy).then_inc(done, 1)
        act.wait_ge(dve, d0 + 3)
        act.activation(tile(EUK), tile(EUK), ACT.Exp).then_inc(done, 1)
        yield
        if w == 0:
            act.wait_ge(in_x0 if b < 2 else in_x1, 16)
            act.wait_ge(dve, d0 + 7)
            act.wait_ge(pool, p0 + 2)
            act.activation(tile(EK), cols(xT, b), ACT.Exp, scale=-1.0).then_inc(done, 1)
            act.wait_ge(done, a0 + 3)
            act.activation(tile(EK), tile(EK), ACT.Copy, bias=1.0).then_inc(done, 1)
            yield
            act.wait_ge(dve, d0 + COND1_DVE[b])
            act.activation(cols(y_hi, b), tile(NB), ACT.Copy).then_inc(yhi_done, 1)
            yield

    def cond_pool(pool, b, w):
        tile, (dve, act, done), (d0, a0, p0) = steps_of(b, w)
        f = keys(b) if w == 0 else VCOPY
        if w == 1:
            pool.wait_ge(act, a0 + 2)
        pool.wait_ge(act, a0 + 1)
        pool.tensor_tensor(tile(EKV), tile(EK), f, ALU.mult).then_inc(done, 1)
        pool.wait_ge(act, a0 + 2 + w)
        pool.tensor_tensor(tile(EUK), tile(EUK), tile(EK), ALU.subtract).then_inc(done, 1)
        yield
        n = p0 + 2
        if sums_on(b, w) == "tensor":
            pool.wait_ge(done, p0 + 2)
            pool.tensor_tensor(spare, tile(EUK), f, ALU.mult).then_inc(done, 1)
            yield
            return
        if sums_on(b, w) == "gpsimd":
            pool.wait_ge(dve, d0 + 7)
            pool.tensor_tensor(tile(DF), tile(DF), tile(DB), ALU.add).then_inc(done, 1)
            pool.wait_ge(done, n + 1)
            pool.tensor_tensor(tile(DF), tile(DF), tile(EUK), ALU.add).then_inc(done, 1)
            n += 2
            yield
        pool.wait_ge(dve, d0 + 11)
        pool.tensor_tensor(tile(NF), tile(NF), tile(NB), ALU.add).then_inc(done, 1)
        pool.wait_ge(done, p0 + 2)
        pool.tensor_tensor(tile(EKV), tile(EUK), f, ALU.mult).then_inc(done, 1)
        pool.wait_ge(done, n + 2)
        pool.tensor_tensor(tile(NF), tile(NF), tile(EKV), ALU.add).then_inc(done, 1)
        yield
        if w == 0:
            pool.wait_ge(yhi_done, b + 1)
            pool.tensor_tensor(cols(y_lo, b), tile(NB), cols(y_hi, b).bitcast(F32), ALU.subtract).then_inc(ylo_done, 1)
            yield

    def weights_of(kind, h=None):
        if kind == "qk":
            return lambda t: t[:, SLOT_Q:SLOT_K + 1, :, h * DH:(h + 1) * DH]
        return lambda t: t[:, SLOT_V if kind == "v" else SLOT_O]

    @block.gpsimd
    def _(pool):
        pool.memset(identf[:], 0.0).then_inc(const_step, 1)
        pool.memset(ident16[:], 0.0).then_inc(const_step, 1)
        pool.memset(identb[:], 0.0).then_inc(const_step, 1)
        pool.memset(negmask[:], 0.0).then_inc(const_step, 1)
        pool.wait_ge(const_step, 4)
        for m in (identf, ident16, identb):
            pool.affine_select(out=m[:], in_=m[:], compare_op=ALU.not_equal, fill=1.0, base=0,
                               pattern=[[-1, P]], channel_multiplier=1).then_inc(consts, 1)
        pool.affine_select(out=negmask[:], in_=negmask[:], compare_op=ALU.is_ge, fill=MASKED, base=0,
                           pattern=[[-1, P]], channel_multiplier=1).then_inc(consts, 1)
        pool.memset(pT[:, :, :, 0:P].bitcast(F32), 0.0).then_inc(consts, 1)
        for e in range(E):
            pool.memset(iota[:, e:e + 1], float(e)).then_inc(consts, 1)

        def refill(kind, g, h=None):
            view = weights_of(kind, h)
            hi, lo = {"v": (whi_v, wlo_v), "qk": (whi_qk, wlo_qk), "o": (whi_o, wlo_o)}[kind]
            pool.wait_ge(hi, (g * GH + h if kind == "qk" else g) + 1)
            pool.tensor_tensor(view(w_lo), view(raw), view(w_hi).bitcast(F32), ALU.subtract).then_inc(lo, 1)

        c = [cond_pool(pool, b, 0) for b in range(B)]
        next(c[0])
        next(c[1])
        next(c[0])
        next(c[1])
        refill("v", 0)
        next(c[0])
        refill("qk", 0, 0)
        refill("qk", 0, 1)
        next(c[2])
        next(c[3])
        refill("qk", 0, 2)
        next(c[2])
        next(c[2])
        refill("qk", 0, 3)
        next(c[3])
        next(c[2])
        next(c[3])
        next(c[3])

        def group(g):
            if not isinstance(g, int):
                for _ in cond_pool(pool, g, 1):
                    pass
            refill("o", g)
            refill("v", g + 1)
            refill("qk", g + 1, 0)
            refill("qk", g + 1, 1)
            if isinstance(g, int) and g == 0:
                for _ in cond_pool(pool, 0, 1):
                    pass
            refill("qk", g + 1, 2)
            refill("qk", g + 1, 3)

        group(0)
        with pool.Fori(1, GROUPS) as g:
            group(g)
        refill("o", GROUPS)

    @block.scalar
    def _(act):
        act.wait_ge(in_small, 32)
        act.activation(ew[:], wu[:, 0:4:2], ACT.Exp).then_inc(pre_act, 1)
        act.wait_ge(pre_act, 1)
        act.activation(ew[:], ew[:], ACT.Exp, scale=-1.0).then_inc(pre_act, 1)
        act.wait_ge(pre_dve, 1)
        act.activation(tf[:], tsum[:], ACT.Exp, scale=-1.0).then_inc(pre_act, 1)

        def refill(kind, g, h=None, freed=None):
            view = weights_of(kind, h)
            landed, hi = {"v": (raw_v, whi_v), "qk": (raw_qk, whi_qk), "o": (raw_o, whi_o)}[kind]
            act.wait_ge(landed, g * 16 + 16)
            if freed is not None:
                act.wait_ge(*freed)
            act.activation(view(w_hi), view(raw), ACT.Copy).then_inc(hi, 1)

        def project_hi(out, i, bank):
            act.wait_ge(projected, i + 1)
            act.activation(out, psA[bank][:], ACT.Copy).then_inc(proj_hi, 1)

        c = [cond_act(act, b, 0) for b in range(B)]
        next(c[0])
        next(c[1])
        refill("v", 0)
        next(c[0])
        refill("qk", 0, 0)
        next(c[1])
        for h in range(1, GH):
            refill("qk", 0, h)
        next(c[0])
        refill("o", 0)
        next(c[1])
        for t in range(2):
            project_hi(v_hi[:, 0, t], t, proj_bank(t))
        next(c[2])
        project_hi(v_hi[:, 0, 2], 2, proj_bank(2))
        next(c[3])
        project_hi(v_hi[:, 0, 3], 3, proj_bank(3))
        for j in range(2):
            project_hi(qk_hi[:, 0, j], TB + j, proj_bank(TB + j))
        next(c[2])
        next(c[3])

        def transposed_copy(g, k):
            act.wait_ge(transposed, g * UNITS_GROUP + k + 1)
            act.activation(pT[:, k % 2, :, P:4 * P], psT[:, 0:6 * P].rearrange("p (a n) -> p a n", a=2),
                           ACT.Copy).then_inc(pT_ready, 1)

        def z_high(h, i, bank):
            act.wait_ge(zo_done, i + 1)
            act.activation(z_hi[:, h], psZ[bank][:], ACT.Copy, scale=1.0 / LIFT).then_inc(z_hi_done, 1)

        def group(g, plan, extra):
            for s in plan:
                hd, par = s["hd"], (s["hd"] + 1) % 2
                if s["prev"]:
                    transposed_copy(g, s["prev_units"][0])
                act.wait_ge(ntopped, g * HEADS + hd + 1)
                for k in (0, 1):
                    act.activation(prob[:, k, 0:P], psS[k][:, 0:P], ACT.Exp, scale=SCALE,
                                   bias=ntop[:, k, 0:1], accum_out=ssum[:, k, 0:1])
                    act.activation(prob[:, k, P:3 * P], psS[k][:, 2 * P:4 * P], ACT.Exp, scale=SCALE,
                                   bias=ntop[:, k, 1:2], accum_out=ssum[:, k, 1:2]).then_inc(exped, 1)
                if s["next_qk"]:
                    project_hi(qk_hi[:, par, 0], proj_base(g) + s["q"], proj_bank(s["q"]))
                if s["next_qk"]:
                    project_hi(qk_hi[:, par, 1], proj_base(g) + s["k"], proj_bank(s["k"]))
                if s["prev"]:
                    transposed_copy(g, s["prev_units"][1])
                for f in extra.get((s["p"], s["h"], "a"), ()):
                    f()

                def z():
                    if s["prev"]:
                        z_high(s["prev_h"], zo_base(g) + s["z"], zo_bank(s["z"]))

                if s["h"] == 0:
                    z()
                for t, i in s["v"]:
                    project_hi(v_hi[:, 1 - s["p"], t], proj_base(g) + i, proj_bank(i))
                if s["h"]:
                    z()
                for f in extra.get((s["p"], s["h"], "c"), ()):
                    f()

        def extras(g, plan):
            first = isinstance(g, int) and g == 0
            c2 = cond_act(act, g, 1)
            out = {
                (1, 0, "a"): [lambda: refill("v", g + 1, freed=(projected, proj_base(g) + last_event(plan, 0, "v") + 1))],
                (1, 0, "c"): [lambda: refill("qk", g + 1, 0, (projected, proj_base(g) + plan[3]["k"] + 1))],
                (1, 1, "a"): [lambda: refill("qk", g + 1, 1, (projected, proj_base(g) + plan[4]["k"] + 1))],
                (1, 2, "a"): [lambda: refill("qk", g + 1, 2, (projected, proj_base(g) + plan[5]["k"] + 1))],
                (1, 3, "a"): [lambda: refill("qk", g + 1, 3, (projected, proj_base(g) + plan[6]["k"] + 1))],
            }
            if first:
                out[(0, 1, "a")] = [lambda: next(c[2])]
                out[(0, 2, "c")] = [lambda: next(c[3])]
                out[(1, 0, "a")].append(lambda: next(c2))
            else:
                out[(0, 0, "a")] = [lambda: next(c2)]
                out[(0, 2, "a")] = [lambda: refill("o", g, freed=(zo_done, zo_base(g) + MIDDLE[1]["o"][-1][1] + 1))]
            if plan is LAST:
                out[(1, 2, "a")] = out.get((1, 2, "a"), []) + [lambda: y2_sigmoid(0), lambda: y2_sigmoid(1)]
                out[(1, 2, "c")] = out.get((1, 2, "c"), []) + [lambda: y2_hi(0), lambda: y2_hi(1)]
            return out

        def y2_sigmoid(b):
            act.wait_ge(zo_read, ZO_X0 if b < 2 else ZO_TOTAL + CB)
            act.activation(cols(y2, b), cols(xT, b), ACT.Sigmoid).then_inc(sigmoid2, 1)

        def y2_hi(b):
            act.wait_ge(y2_done, b + 1)
            act.wait_ge(projected, proj_base(GROUPS - 1) + LAST[2]["k"] + 1 if b < 2 else PROJ_TOTAL)
            act.activation(cols(y_hi, b), cols(y2, b), ACT.Copy).then_inc(y2hi_done, 1)

        group(0, FIRST, extras(0, FIRST))
        with act.Fori(1, GROUPS - 1) as g:
            group(g, MIDDLE, extras(g, MIDDLE))
        group(GROUPS - 1, LAST, extras(GROUPS - 1, LAST))

        def gate_softmax(p):
            act.wait_ge(gate_step, p * GATE_STEPS + 2 + 2 * TB)
            act.activation(gw2[:], gap[:], ACT.Sigmoid).then_inc(gate_soft, 1)
            act.activation(gw1[:], gap[:], ACT.Sigmoid, scale=-1.0).then_inc(gate_soft, 1)

        def gates_copy(p):
            act.wait_ge(gT_done, p + 1)
            act.activation(gatesT[:, p], psG[0:E, :], ACT.Copy).then_inc(gT_copied, 1)

        def base_copies(p):
            for k in range(2):
                act.wait_ge(based, 2 * p + k + 1)
                act.activation(acc[:, p * TB + 2 * k:p * TB + 2 * k + 2],
                               psB[k][:].rearrange("p (a n) -> p a n", a=2), ACT.Copy).then_inc(base_copied, 1)

        gate_softmax(0)
        for k in (-2, -1):
            transposed_copy(GROUPS, k)
        gates_copy(0)
        z_high(GH - 1, ZO_UNITS, zo_bank(ZO_GROUP))
        base_copies(0)
        for b in range(2, 4):
            y2_sigmoid(b)
        refill("o", GROUPS, freed=(zo_done, ZO_TOTAL + CB))
        for b in range(2, 4):
            y2_hi(b)
        gate_softmax(1)
        gates_copy(1)
        base_copies(1)

    @block.vector
    def _(dve):
        dve.wait_ge(in_small, 32)
        dve.tensor_reduce(tsum[:], temb[:], AX.X, ALU.add).then_inc(pre_dve, 1)
        dve.wait_ge(pre_act, 3)
        dve.tensor_scalar(tf[:], tf[:], 1.0, None, ALU.add).then_inc(pre_dve, 1)
        dve.wait_ge(pre_dve, 2)
        dve.reciprocal(tf[:], tf[:]).then_inc(pre_dve, 1)
        dve.wait_ge(pre_dve, 3)
        dve.tensor_scalar(tdec[:], tf[:], 0.5, 0.5, ALU.mult, ALU.add).then_inc(pre_dve, 1)
        dve.tensor_scalar(tout[:], tf[:], 0.2, 0.8, ALU.mult, ALU.add).then_inc(pre_dve, 1)
        dve.wait_ge(pre_dve, 5)
        for w in range(2):
            for c in range(CB):
                dve.tensor_scalar(decay[:, w, c], tdec[:], ew[:, w, c:c + 1], None, ALU.mult).then_inc(pre_dve, 1)
        dve.wait_ge(pre_dve, 9)

        def project_lo(out, hi, i, bank):
            dve.wait_ge(proj_hi, i + 1)
            dve.tensor_tensor(out, psA[bank][:], hi.bitcast(F32), ALU.subtract).then_inc(proj_lo, 1)

        c = [cond_dve(dve, b, 0) for b in range(B)]
        for b in (0, 1, 0, 1, 0, 0, 0, 0, 0, 1, 1, 1, 1):
            next(c[b])
        dve.wait_ge(ylo_done, 1)
        dve.wait_ge(yhi_done, 2)
        dve.tensor_tensor(cols(y_lo, 1), tiles[:, 1, NB], cols(y_hi, 1).bitcast(F32), ALU.subtract).then_inc(ylo_done, 1)
        for t, stage in zip(range(TB), (2, 3, 2, 2)):
            project_lo(v_lo[:, 0, t], v_hi[:, 0, t], t, proj_bank(t))
            next(c[stage])
        for j in range(2):
            project_lo(qk_lo[:, 0, j], qk_hi[:, 0, j], TB + j, proj_bank(TB + j))
        next(c[3])

        def maxima(g, hd):
            for k in (0, 1):
                dve.wait_ge(scored, g * UNITS_GROUP + 2 * hd + k + 1)
                dve.tensor_reduce(top[:, k, 0:1], psS[k][:, 0:P], AX.X, ALU.max).then_inc(topped, 1)
                dve.tensor_reduce(top[:, k, 1:2], psS[k][:, 2 * P:4 * P], AX.X, ALU.max).then_inc(topped, 1)
            dve.wait_ge(topped, 4 * (g * HEADS + hd + 1))
            dve.tensor_scalar(ntop[:], top[:], -SCALE, None, ALU.mult).then_inc(ntopped, 1)

        def sums(g, hd):
            dve.wait_ge(exped, 2 * (g * HEADS + hd + 1))
            dve.tensor_scalar(ssmall[:], ssum[:], 1.0 / LIFT, None, ALU.mult).then_inc(summed, 1)

        def reciprocals(g, hd):
            dve.wait_ge(summed, g * HEADS + hd + 1)
            dve.reciprocal(rsum[:], ssmall[:]).then_inc(recipd, 1)

        ROWS = ((slice(0, P), 0), (slice(P, 3 * P), 1))

        def high_part(g, hd, k):
            if k == 0:
                dve.wait_ge(recipd, g * HEADS + hd + 1)
            if not (isinstance(g, int) and g == 0 and hd == 0):
                dve.wait_ge(transposed, g * UNITS_GROUP + 2 * hd + k - 1)
            for c, q in ROWS:
                dve.tensor_scalar(prob16[:, k, 0, c], prob[:, k, c], rsum[:, k, q:q + 1], None, ALU.mult).then_inc(halved_hi, 1)

        def low_part(g, hd, k):
            dve.wait_ge(halved_hi, 2 * (g * UNITS_GROUP + 2 * hd + k) + 2)
            for c, q in ROWS:
                dve.scalar_tensor_tensor(prob16[:, k, 1, c], prob[:, k, c], rsum[:, k, q:q + 1], prob16[:, k, 0, c],
                                         ALU.mult, ALU.subtract).then_inc(halved, 1)

        def add_output(p, c, i, bank):
            dve.wait_ge(zo_done, i + 1)
            dve.wait_ge(zo_read, i)
            x = xT[:, c, p * PAIR:(p + 1) * PAIR]
            dve.tensor_tensor(x, psZ[bank][:], x, ALU.add).then_inc(zo_read, 1)

        def z_low(h, n, bank):
            dve.wait_ge(z_hi_done, n)
            dve.scalar_tensor_tensor(z_lo[:, h], psZ[bank][:], 1.0 / LIFT, z_hi[:, h].bitcast(F32),
                                     ALU.mult, ALU.subtract).then_inc(zo_read, 1)

        def group(g, plan, extra):
            for s in plan:
                hd, par = s["hd"], (s["hd"] + 1) % 2
                maxima(g, hd)
                if hd > 1:
                    z_low((hd - 2) % GH, g * HEADS + hd - 1, zo_bank(plan[hd - 1]["z"]))
                elif not (isinstance(g, int) and g == 0):
                    z_low((hd - 2) % GH, g * HEADS + hd - 1, zo_bank(plan[hd - 1]["z"] if hd else -1))
                for f in extra.get((s["p"], s["h"], "m"), ()):
                    f()
                if s["next_qk"]:
                    project_lo(qk_lo[:, par, 0], qk_hi[:, par, 0], proj_base(g) + s["q"], proj_bank(s["q"]))
                sums(g, hd)
                if s["next_qk"]:
                    project_lo(qk_lo[:, par, 1], qk_hi[:, par, 1], proj_base(g) + s["k"], proj_bank(s["k"]))
                reciprocals(g, hd)
                high_part(g, hd, 0)
                high_part(g, hd, 1)
                low_part(g, hd, 0)
                low_part(g, hd, 1)
                outputs = [lambda c=c, i=i: add_output(1 - s["p"], c, zo_base(g) + i, zo_bank(i)) for c, i in s["o"]]
                for f in outputs[:1] + extra.get((s["p"], s["h"], "a"), []) + outputs[1:]:
                    f()
                for t, i in s["v"]:
                    project_lo(v_lo[:, 1 - s["p"], t], v_hi[:, 1 - s["p"], t], proj_base(g) + i, proj_bank(i))
                for f in extra.get((s["p"], s["h"], "c"), ()):
                    f()

        def extras(g, plan):
            c2 = cond_dve(dve, g, 1)
            n2 = lambda: next(c2)
            if isinstance(g, int) and g == 0:
                n0, n1 = lambda: next(c[2]), lambda: next(c[3])
                out = {(0, 0, "m"): [n0], (0, 0, "a"): [n0], (0, 1, "m"): [n0, n1], (0, 1, "c"): [n1], (0, 2, "m"): [n1], (0, 2, "a"): [n1],
                       (1, 0, "m"): [n2], (1, 1, "m"): [n2], (1, 1, "a"): [n2],
                       (1, 2, "m"): [n2], (1, 3, "m"): [n2], (1, 3, "c"): [n2]}
            else:
                out = {(0, 0, "m"): [n2], (0, 1, "m"): [n2], (0, 2, "m"): [n2],
                       (1, 0, "m"): [n2], (1, 1, "m"): [n2], (1, 1, "a"): [n2]}
            if plan is LAST:
                out[(1, 2, "c")] = out.get((1, 2, "c"), []) + [lambda: y2_product(0), lambda: y2_product(1)]
                out[(1, 3, "m")] = out.get((1, 3, "m"), []) + [lambda: y2_lo(0), lambda: y2_lo(1)]
            return out

        def y2_product(b):
            dve.wait_ge(sigmoid2, b + 1)
            dve.wait_ge(c2_dve, (b + 1) * COND2_DVE)
            dve.tensor_tensor(cols(y2, b), cols(y2, b), cols(ratio2, b), ALU.mult).then_inc(y2_done, 1)

        def y2_lo(b):
            dve.wait_ge(y2hi_done, b + 1)
            dve.tensor_tensor(cols(y_lo, b), cols(y2, b), cols(y_hi, b).bitcast(F32), ALU.subtract).then_inc(y2lo_done, 1)

        group(0, FIRST, extras(0, FIRST))
        with dve.Fori(1, GROUPS - 1) as g:
            group(g, MIDDLE, extras(g, MIDDLE))
        group(GROUPS - 1, LAST, extras(GROUPS - 1, LAST))
        z_low(GH - 2, GROUPS * HEADS - 1, zo_bank(-1))

        def gate(p):
            n = [p * GATE_STEPS]

            def step(ins):
                n[0] += 1
                ins.then_inc(gate_step, 1)

            dve.wait_ge(logits_done, p + 1)
            if p:
                dve.wait_ge(gates_done, p)
            step(dve.tensor_copy(logit[:].rearrange("p t e -> p (t e)"), psG[:, 0:TB * E]))
            dve.wait_ge(gate_step, n[0])
            for t in range(TB):
                step(dve.max(best[:, t], logit[:, t]))
            dve.wait_ge(gate_step, n[0])
            for t in range(TB):
                step(dve.max_index(besti[:, t], best[:, t], logit[:, t]))
            step(dve.tensor_tensor(gap[:], best[:, :, 1], best[:, :, 0], ALU.subtract))
            dve.wait_ge(gate_step, n[0])
            step(dve.tensor_copy(bestf[:], besti[:]))
            dve.wait_ge(gate_soft, 2 * p + 2)
            dve.wait_ge(gate_step, n[0])
            for t in range(TB):
                step(dve.tensor_scalar(gates[:, p, t], iota[:], bestf[:, t, 0:1], gw1[:, t:t + 1], ALU.is_equal, ALU.mult))
                step(dve.tensor_scalar(gsec[:, t], iota[:], bestf[:, t, 1:2], gw2[:, t:t + 1], ALU.is_equal, ALU.mult))
            dve.wait_ge(gate_step, n[0])
            dve.tensor_tensor(gates[:, p], gates[:, p], gsec[:], ALU.add).then_inc(gates_done, 1)

        def add_experts(j):
            p, slot, t = j // (4 * TB), j // TB % 4, j % TB
            a = acc[:, p * TB + t]
            dve.wait_ge(base_copied, 2 * p + t // 2 + 1)
            dve.wait_ge(expert_done, j + 1)
            if slot:
                dve.wait_ge(expert_read, j - TB + 1)
            for e in range(2):
                if e:
                    dve.wait_ge(expert_half, j + 1)
                ins = dve.scalar_tensor_tensor(a, psE[j % 4][:, e * C:(e + 1) * C], gates[:, p, t, 2 * slot + e:2 * slot + e + 1],
                                               a, ALU.mult, ALU.add)
                ins.then_inc(expert_read if e else expert_half, 1)

        gate(0)
        z_low(GH - 1, GROUPS * HEADS, zo_bank(ZO_GROUP))
        work = {1: [lambda c=c: add_output(1, c, ZO_TOTAL + c, zo_bank(ZO_GROUP + 1 + c)) for c in range(CB)],
                3: [lambda: y2_product(2), lambda: y2_product(3)],
                6: [lambda: y2_lo(2), lambda: y2_lo(3)], 10: [lambda: gate(1)]}
        for j in range(8 * TB):
            add_experts(j)
            for f in work.get(j, ()):
                f()

    @block.tensor
    def _(pe):
        def three(out, pairs, start=True, stop=True):
            n = len(pairs)
            for k, ((ah, al), (bh, bl)) in enumerate(pairs):
                pe.matmul(out, ah, bh, start=start and k == 0, stop=False)
                pe.matmul(out, ah, bl, start=False, stop=False)
                ins = pe.matmul(out, al, bh, start=False, stop=stop and k == n - 1)
            return ins

        def both(hi, lo, *index):
            return hi[index], lo[index]

        def bank_free(i):
            if not (isinstance(i, int) and i < 3):
                pe.wait_ge(proj_lo, i - 2)

        def project_qk(j, h, p, i, bank):
            bank_free(i)
            three(psA[bank][:], [(both(w_hi, w_lo, slice(None), SLOT_Q + j, c, slice(h * DH, (h + 1) * DH)),
                                  both(y_hi, y_lo, slice(None), c, slice(p * PAIR, (p + 1) * PAIR)))
                                 for c in range(CB)]).then_inc(projected, 1)

        def project_v(t, p, i, bank):
            bank_free(i)
            k = p * PAIR + t * P
            three(psA[bank][:], [(both(y_hi, y_lo, slice(None), c, slice(k, k + P)),
                                  both(w_hi, w_lo, slice(None), SLOT_V, c)) for c in range(CB)]).then_inc(projected, 1)

        def scores(g, k, par):
            b = k % 2
            if not (isinstance(g, int) and g * UNITS_GROUP + k < 2):
                pe.wait_ge(exped, g * UNITS_GROUP + k - 1)
            for q in range(2):
                out, tokens = psS[b][:, q * T:(q + 1) * T], slice(b * T + q * P, b * T + q * P + P)
                keys_hi, keys_lo = (t[:, par, 1, b * T:(b + 1) * T] for t in (qk_hi, qk_lo))
                pe.matmul(out, qk_hi[:, par, 0, tokens], keys_hi, start=True, stop=False)
                pe.matmul(out, qk_hi[:, par, 0, tokens], keys_lo, start=False, stop=False)
                pe.matmul(out[:, q * P:(q + 1) * P], identb[:], negmask[:], start=False, stop=False)
                ins = pe.matmul(out, qk_lo[:, par, 0, tokens], keys_hi, start=False, stop=True)
            ins.then_inc(scored, 1)

        def transposes(g, k):
            u = k % 2
            pe.wait_ge(halved, 2 * (g * UNITS_GROUP + k + 1))
            if not (isinstance(g, int) and g * UNITS_GROUP + k < 1):
                pe.wait_ge(pT_ready, g * UNITS_GROUP + k)
            for part in range(2):
                for n, c in enumerate((2, 0, 1)):
                    o = (part * 3 + n) * P
                    ins = pe.transpose(psT[:, o:o + P], prob16[:, u, part, c * P:(c + 1) * P], ident16[:])
            ins.then_inc(transposed, 1)

        def zo_free(i):
            if not (isinstance(i, int) and i < 2):
                pe.wait_ge(zo_read, i - 1)

        def values(n, h, p, i, bank):
            zo_free(i)
            for b in range(2):
                pe.wait_ge(pT_ready, n + b + 1)
                ins = three(psZ[bank][:, b * T:(b + 1) * T],
                            [(both(v_hi, v_lo, slice(None), p, 2 * b + kb, slice(h * DH, (h + 1) * DH)),
                              (pT[:, b, 0, (1 - kb) * T:(2 - kb) * T], pT[:, b, 1, (1 - kb) * T:(2 - kb) * T]))
                             for kb in range(2)])
            ins.then_inc(zo_done, 1)

        def output(c, i, bank):
            zo_free(i)
            pe.wait_ge(zo_read, i - c)
            three(psZ[bank][:], [(both(w_o_hi, w_o_lo, slice(None), h, slice(c * P, (c + 1) * P)),
                                  both(z_hi, z_lo, slice(None), h)) for h in range(GH)]).then_inc(zo_done, 1)

        w_o_hi = w_hi[:, SLOT_O].rearrange("p c n -> p (c n)").rearrange("p (h n) -> p h n", h=GH)
        w_o_lo = w_lo[:, SLOT_O].rearrange("p c n -> p (c n)").rearrange("p (h n) -> p h n", h=GH)

        pe.wait_ge(consts, 1)
        t1 = tiles[:, 1]
        for bank, parts, scans in ((0, (t1[:, DF], t1[:, DB], t1[:, EUK]), 7), (1, (spare, t1[:, NF], t1[:, NB]), 11)):
            pe.wait_ge(c1_dve[1], scans)
            pe.wait_ge(c1_pool[1], 2 + bank)
            for k, part in enumerate(parts):
                ins = pe.matmul(psSum[bank][:], identf[:], part,
                                start=k == 0, stop=k == len(parts) - 1)
            ins.then_inc(summed_pe, 1)
        pe.wait_ge(wlo_v, 1)
        for t in range(TB):
            pe.wait_ge(yhi_done, t // 2 + 1)
            pe.wait_ge(ylo_done, t // 2 + 1)
            project_v(t, 0, t, proj_bank(t))
        pe.wait_ge(wlo_qk, 1)
        for j in range(2):
            project_qk(j, 0, 0, TB + j, proj_bank(TB + j))
        pe.wait_ge(consts, 5 + E)
        pe.wait_ge(c1_dve[1], COND1_DVE[1])

        def group(g, plan):
            for s in plan:
                p, h, par = s["p"], s["h"], s["hd"] % 2
                units = (2 * s["hd"], 2 * s["hd"] + 1)
                if s["hd"]:
                    pe.wait_ge(proj_lo, proj_base(g) + plan[s["hd"] - 1]["k"] + 1)
                elif isinstance(g, int) and g == 0:
                    pe.wait_ge(proj_lo, PROJ_AHEAD)
                else:
                    pe.wait_ge(proj_lo, proj_base(g) - PROJ_GROUP + MIDDLE[-1]["k"] + 1)
                nh, np_ = (h + 1) % GH, (p if h < GH - 1 else 1 - p)
                ng = g if s["hd"] < HEADS - 1 else g + 1
                for k in units:
                    scores(g, k, par)
                if s["prev"]:
                    transposes(g, s["prev_units"][0])
                if s["next_qk"]:
                    pe.wait_ge(wlo_qk, ng * GH + nh + 1)
                    if isinstance(g, int) and g == 0 and p == 0 and h == GH - 1:
                        pe.wait_ge(yhi_done, 4)
                        pe.wait_ge(ylo_done, 4)
                    project_qk(0, nh, np_, proj_base(g) + s["q"], proj_bank(s["q"]))
                if s["next_qk"]:
                    project_qk(1, nh, np_, proj_base(g) + s["k"], proj_bank(s["k"]))
                if not s["next_qk"]:
                    logits(0)
                if s["prev"]:
                    transposes(g, s["prev_units"][1])
                for c, i in s["o"]:
                    pe.wait_ge(wlo_o, g + (1 if p == 1 else 0))
                    output(c, zo_base(g) + i, zo_bank(i))

                def z():
                    if s["prev"]:
                        values(g * UNITS_GROUP + s["prev_units"][0], s["prev_h"], s["prev_p"],
                               zo_base(g) + s["z"], zo_bank(s["z"]))

                if h == 0:
                    z()
                for t, i in s["v"]:
                    if isinstance(g, int) and g == 0 and p == 0:
                        pe.wait_ge(yhi_done, 3 + t // 2)
                        pe.wait_ge(ylo_done, 3 + t // 2)
                    pe.wait_ge(wlo_v, g + 1 + p)
                    project_v(t, 1 - p, proj_base(g) + i, proj_bank(i))
                if h:
                    z()

        def logits(p):
            pe.wait_ge(in_late, 32)
            pe.wait_ge(y2_done, 2 * p + 2)
            if p == 0:
                pe.wait_ge(proj_lo, PROJ_TOTAL)
            else:
                pe.wait_ge(gT_copied, p)
            for t in range(TB):
                for c in range(CB):
                    n = p * PAIR + t * P
                    ins = pe.matmul(psG[:, t * E:(t + 1) * E], y2[:, c, n:n + P], gate_w[:, c], start=c == 0, stop=c == CB - 1)
            ins.then_inc(logits_done, 1)

        def gates_turn(p):
            pe.wait_ge(gates_done, p + 1)
            if p:
                pe.wait_ge(gT_copied, p)
            for t in range(TB):
                ins = pe.transpose(psG[0:E, t * P:(t + 1) * P], gates[:, p, t], identf[:])
            ins.then_inc(gT_done, 1)

        def base(p):
            pe.wait_ge(gT_copied, p + 1)
            if p == 0:
                pe.wait_ge(exped, GROUPS * UNITS_GROUP)
            else:
                pe.wait_ge(base_copied, 2 * p)
            for k in range(2):
                for tt in range(2):
                    t = 2 * k + tt
                    n = p * PAIR + t * P
                    for c in range(CB):
                        o = psB[k][:, tt * C + c * P:tt * C + (c + 1) * P]
                        pe.matmul(o, gatesT[:, p, t * P:(t + 1) * P], expert_b[:, c * P:(c + 1) * P], start=True, stop=False)
                        ins = pe.matmul(o, xT[:, c, n:n + P], identf[:], start=False, stop=True)
                ins.then_inc(based, 1)

        def experts(j):
            p, slot, t = j // (4 * TB), j // TB % 4, j % TB
            if j >= 4:
                pe.wait_ge(expert_read, j - 3)
            elif j < 2:
                pe.wait_ge(proj_lo, PROJ_TOTAL)
            else:
                pe.wait_ge(zo_read, ZO_TOTAL + j - 1)
            if j < 4 * TB:
                if slot == 0:
                    pe.wait_ge(wlo_v, GROUPS + 1)
                elif slot < 3:
                    pe.wait_ge(wlo_qk, (GROUPS + 1) * GH)
                else:
                    pe.wait_ge(wlo_o, GROUPS + 1)
            pe.wait_ge(y2lo_done, 2 * p + t // 2 + 1)
            n = p * PAIR + t * P
            three(psE[j % 4][:], [(both(y_hi, y_lo, slice(None), c, slice(n, n + P)),
                                both(w_hi, w_lo, slice(None), EXPERT_SLOTS[slot], c)) for c in range(CB)]).then_inc(expert_done, 1)

        group(0, FIRST)
        with pe.Fori(1, GROUPS - 1) as g:
            group(g, MIDDLE)
        group(GROUPS - 1, LAST)
        for j in range(2):
            experts(j)
            transposes(GROUPS, j - 2)
        gates_turn(0)
        values(GROUPS * UNITS_GROUP - 2, GH - 1, NPAIR - 1, ZO_UNITS, zo_bank(ZO_GROUP))
        base(0)
        pe.wait_ge(wlo_o, GROUPS)
        for c in range(CB):
            output(c, ZO_TOTAL + c, zo_bank(ZO_GROUP + 1 + c))
        for j in range(2, 8 * TB):
            experts(j)
            if j == 9:
                logits(1)
            if j == 13:
                gates_turn(1)
            if j == 14:
                base(1)
    return None


def lay_out(inputs):
    import numpy as np

    def channels_first(a):
        return np.ascontiguousarray(a.reshape(N, CB, P).transpose(2, 1, 0))

    def by_channel(a):
        return a.reshape(a.shape[0], CB, P).transpose(2, 1, 0)

    weights = np.empty((GROUPS + 1, P, 4, CB, GH * DH), np.float32)
    for slot, name in ((SLOT_Q, "L0_attn_W_Q"), (SLOT_K, "L0_attn_W_K"), (SLOT_V, "L0_attn_W_V")):
        w = inputs[name]
        for g in range(GROUPS):
            weights[g, :, slot] = by_channel(w[g * GH:(g + 1) * GH].reshape(GH * DH, C))
    wo = inputs["L0_attn_W_O"].reshape(C, GROUPS, GH, DH).transpose(1, 3, 2, 0)
    weights[:GROUPS, :, SLOT_O] = wo.reshape(GROUPS, P, CB, GH * DH)
    we = inputs["L0_ffn_expert_w"].reshape(4, 2, CB, P, C).transpose(0, 3, 2, 1, 4)
    for k, slot in enumerate(EXPERT_SLOTS):
        weights[GROUPS, :, slot] = we[k].reshape(P, CB, GH * DH)
    wu = np.stack([inputs[n].reshape(CB, P).T for n in ("L0_cond_w", "L0_cond_u", "L0_cond2_w", "L0_cond2_u")], 1)
    return {
        "xT": channels_first(inputs["x"]),
        "fT": channels_first(inputs["fside_BxSxS_0"]),
        "temb": np.ascontiguousarray(inputs["cond_512"]),
        "wu": np.ascontiguousarray(wu),
        "weights": weights,
        "gate_w": np.ascontiguousarray(by_channel(inputs["L0_ffn_gate_w"])),
        "expert_b": np.ascontiguousarray(inputs["L0_ffn_expert_b"]),
    }


def kernel(**inputs):
    from contextlib import ExitStack
    import numpy as np
    import concourse.bacc as bacc
    from concourse.bass_utils import run_bass_kernel_spmd

    arrays = lay_out({k: np.asarray(v) for k, v in inputs.items()})
    nc = bacc.Bacc("TRN2", target_bir_lowering=False, num_devices=1)
    aps = {n: nc.dram_tensor("in_" + n, a.shape, F32, kind="ExternalInput").ap() for n, a in arrays.items()}
    aps["out"] = nc.dram_tensor("out", (N, C), F32, kind="ExternalOutput").ap()
    with ExitStack() as ctx:
        build(nc, ctx, aps)
    r = run_bass_kernel_spmd(nc, [{"in_" + n: a for n, a in arrays.items()}], core_ids=[0])
    return r.results[0]["out"].reshape(B, T, C)
```
